# Optimizing a Trainium2 kernel written in Bass

```python
import numpy as np
import jax
import jax.numpy as jnp

def _softmax(x, axis=-1):
    return jax.nn.softmax(x, axis=axis)

def _gelu(x):
    return jax.nn.gelu(x, approximate=True)

def _silu(x):
    return jax.nn.silu(x)

def _sigmoid(x):
    return jax.nn.sigmoid(x)

def _layernorm(x, axis=-1, eps=1e-05):
    m = jnp.mean(x, axis=axis, keepdims=True)
    v = jnp.var(x, axis=axis, keepdims=True)
    return (x - m) / jnp.sqrt(v + eps)

def _scatter_add(tgt, idx, src, axis=0):
    return tgt.at[idx].add(src)

def _segment_sum(src, seg, n):
    return jax.ops.segment_sum(src, seg, n)
kernel_name = 'mk_adaln_d1_jaxref_r4_dd7f69'

def setup_inputs(seed: int=0):
    np.random.seed(seed)
    _w = jnp.asarray

    def _L0_attn_setup():
        import jax, jax.numpy as jnp
        import numpy as np
        BH = 32
        BW = 32
        key = jax.random.key(seed)
        k1, k2, k3, k4 = jax.random.split(key, 4)
        B, S, K, N = (2, 512, 1024, 1024)
        data = jax.random.normal(k1, (B, S, K), dtype=jnp.float32)
        weight = jax.random.normal(k2, (N, K), dtype=jnp.float32) * 0.02
        bias = jax.random.normal(k3, (N,), dtype=jnp.float32) * 0.02
        Nb, Kb = (N // BH, K // BW)
        block_on = jax.random.uniform(k4, (Nb, Kb)) < 0.3
        mask = jnp.repeat(jnp.repeat(block_on, BH, axis=0), BW, axis=1).astype(jnp.int32)
        return {'data': data, 'mask': mask, 'weight': weight, 'bias': bias}
    _L0_attn_in = _L0_attn_setup()

    def _L0_ffn_setup():
        import jax, jax.numpy as jnp
        import numpy as np
        D_MODEL = 1024
        D_FF = 2752

        def _dequant_matmul(x, w_int, s):
            w = w_int.astype(jnp.float32) * s
            return x @ w.T
        key = jax.random.key(seed)
        ks = jax.random.split(key, 7)
        x = jax.random.normal(ks[0], (4, 512, D_MODEL), dtype=jnp.float32)
        gate_w = jax.random.randint(ks[1], (D_FF, D_MODEL), -128, 128, dtype=jnp.int32)
        up_w = jax.random.randint(ks[2], (D_FF, D_MODEL), -128, 128, dtype=jnp.int32)
        down_w = jax.random.randint(ks[3], (D_MODEL, D_FF), -128, 128, dtype=jnp.int32)
        gate_s = jax.random.uniform(ks[4], (D_FF, 1), dtype=jnp.float32) * 0.01
        up_s = jax.random.uniform(ks[5], (D_FF, 1), dtype=jnp.float32) * 0.01
        down_s = jax.random.uniform(ks[6], (D_MODEL, 1), dtype=jnp.float32) * 0.01
        return {'x': x, 'gate_w': gate_w, 'gate_s': gate_s, 'up_w': up_w, 'up_s': up_s, 'down_w': down_w, 'down_s': down_s}
    _L0_ffn_in = _L0_ffn_setup()
    _L0_c = _w((lambda *s: np.random.randn(*s).astype(np.float32) * 0.05)(1, 1024))
    _L0_wmod = _w((lambda *s: np.random.randn(*s).astype(np.float32) * 0.05)(1024, 6 * 1024) * 1024 ** (-0.5))
    _d = {'L0_attn_data': _L0_attn_in['data'], 'L0_attn_mask': _L0_attn_in['mask'], 'L0_attn_weight': _L0_attn_in['weight'], 'L0_attn_bias': _L0_attn_in['bias'], 'L0_ffn_gate_w': _L0_ffn_in['gate_w'], 'L0_ffn_gate_s': _L0_ffn_in['gate_s'], 'L0_ffn_up_w': _L0_ffn_in['up_w'], 'L0_ffn_up_s': _L0_ffn_in['up_s'], 'L0_ffn_down_w': _L0_ffn_in['down_w'], 'L0_ffn_down_s': _L0_ffn_in['down_s'], 'L0_c': _L0_c, 'L0_wmod': _L0_wmod}
    _x0 = _d['L0_attn_data']
    _d['L0_attn_data'] = jax.random.normal(jax.random.fold_in(jax.random.key(seed), 1), (1, 2048, 1024), dtype=_x0.dtype)
    del _x0
    return _d

def reference(L0_attn_data, L0_attn_mask, L0_attn_weight, L0_attn_bias, L0_ffn_gate_w, L0_ffn_gate_s, L0_ffn_up_w, L0_ffn_up_s, L0_ffn_down_w, L0_ffn_down_s, L0_c, L0_wmod):

    def _L0_attn_ref(data, mask, weight, bias):
        import jax, jax.numpy as jnp
        import numpy as np
        BH = 32
        BW = 32
        N, K = weight.shape
        Nb, Kb = (N // BH, K // BW)
        bm = mask.reshape(Nb, BH, Kb, BW).sum(axis=(1, 3)) > 0
        wb = weight.reshape(Nb, BH, Kb, BW) * bm[:, None, :, None].astype(weight.dtype)
        w = wb.reshape(N, K)
        out = jnp.einsum('bsk,nk->bsn', data, w) + bias
        return out

    def _L0_ffn_ref(x, gate_w, gate_s, up_w, up_s, down_w, down_s):
        import jax, jax.numpy as jnp
        import numpy as np
        D_MODEL = 1024
        D_FF = 2752

        def _dequant_matmul(x, w_int, s):
            w = w_int.astype(jnp.float32) * s
            return x @ w.T
        batch, seq_len, hidden = x.shape
        x_flat = x.reshape(-1, hidden).astype(jnp.float32)
        gate = _dequant_matmul(x_flat, gate_w, gate_s)
        up = _dequant_matmul(x_flat, up_w, up_s)
        h = jax.nn.silu(gate) * up
        out = _dequant_matmul(h, down_w, down_s)
        return out.astype(x.dtype).reshape(batch, seq_len, hidden)
    x = L0_attn_data
    mod = (_silu(L0_c) @ L0_wmod).reshape(L0_c.shape[0], 6, 1, -1)
    sa, ca, ga, sb, cb, gb = (mod[:, 0], mod[:, 1], mod[:, 2], mod[:, 3], mod[:, 4], mod[:, 5])
    ga = (2 * (ga >= 0) - 1) * jnp.maximum(jnp.abs(ga), 0.25)
    gb = (2 * (gb >= 0) - 1) * jnp.maximum(jnp.abs(gb), 0.25)
    h = _layernorm(x, axis=-1) * (1 + ca) + sa
    x = x + ga * _L0_attn_ref(h, L0_attn_mask, L0_attn_weight, L0_attn_bias)
    h = _layernorm(x, axis=-1) * (1 + cb) + sb
    x = x + gb * _L0_ffn_ref(h, L0_ffn_gate_w, L0_ffn_gate_s, L0_ffn_up_w, L0_ffn_up_s, L0_ffn_down_w, L0_ffn_down_s)
    return x

_drawn_inputs = setup_inputs


def setup_inputs(seed=0):
    import zlib

    import numpy as np

    out = dict(_drawn_inputs(seed))
    spreads = {}
    factors = {'L0_attn_bias': 7.937}
    for name, (base, spread) in spreads.items():
        noise = np.random.default_rng([zlib.crc32(name.encode()), seed]).standard_normal(out[name].shape)
        drawn = base * np.exp(spread * noise) if base else spread * noise
        out[name] = jnp.asarray(drawn.astype(out[name].dtype))
    for name, factor in factors.items():
        out[name] = (out[name] * factor).astype(out[name].dtype)
    return out
```

```python
from contextlib import ExitStack

import concourse.bass as bass
from concourse import mybir

F32 = mybir.dt.float32
F16 = mybir.dt.float16
I32 = mybir.dt.int32
ALU = mybir.AluOpType
ACT = mybir.ActivationFunctionType
AXX = mybir.AxisListType.X

P = 128
EPS = 1e-5
GATE_FLOOR = 0.25


def adaln_kernel(nc, data, mask, weight, bias, gate_w, gate_s, up_w, up_s, down_w, down_s, c_in, wmod, out):
    T, D = data.shape[1], data.shape[2]
    F = gate_w.shape[0]
    Q = 32
    A = P // Q
    KT = D // P
    KA = D // A
    NT = T // P
    H = 512
    FT = F // P
    FL = F - FT * P
    FA = FT * Q
    NF = FT + 1
    assert FL == P // 2 and NF % 2 == 0 and D == 2 * H and KA == KT * Q
    BT = H // P
    NB = T // H
    NQ = 4
    QB = D // Q // NQ
    FC = 3
    CF = FT // FC
    LO = 2048.0
    W_MAX = 128.0

    x_v = data.rearrange("o (n p) d -> (o n) p d", p=P)
    out_v = out.rearrange("o (n p) d -> (o n) p d", p=P)
    x1_d = nc.dram_tensor("x1_scratch", (NT, P, D), F32).ap()
    h_d = nc.dram_tensor("h_scratch", (NT, P, 2 * D), F16).ap()
    h_blk = h_d.rearrange("(b t) p e -> b p t e", t=BT)
    w_v = weight.rearrange("(q b j) (a k) -> q a j b k", q=NQ, j=Q, a=A)
    m_v = mask.rearrange("(q b j) (a k) -> q a j b k", q=NQ, j=Q, a=A)
    gu_v = [w[0:FT * P, :].rearrange("(b q j) (a k) -> q a j b k", b=A, j=Q, a=A) for w in (gate_w, up_w)]
    gu_l = [w[FT * P:F, :].rearrange("(b j) (a k) -> a j b k", j=Q, a=A) for w in (gate_w, up_w)]
    dn_v = down_w[:, 0:FT * P].rearrange("(d b j) (a g k) -> d g a j b k", b=A, j=Q, a=A, g=FC)
    dn_l = down_w[:, FT * P:F].rearrange("(b j) (a k) -> a j b k", j=Q, k=Q)
    mod_v = wmod.rearrange("(p t) n -> p t n", p=P)

    with ExitStack() as ctx:
        ctx.enter_context(nc.allow_non_contiguous_dma(reason="the scales of the weights, once, 22 KB"))
        def sem(name):
            return ctx.enter_context(nc.semaphore(name))

        wgu = ctx.enter_context(nc.sbuf_tensor("wgu", [P, FT * 2 * D + D], F16))
        wgu_u = wgu[:, :].rearrange("p (u e) -> p u e", e=D)
        gbs = ctx.enter_context(nc.sbuf_tensor("gbs", [P, D], F32))
        small = ctx.enter_context(nc.sbuf_tensor("small", [P, 240], F32))
        WORK = nc.sbuf_bytes_remaining // 64 * 64
        work = ctx.enter_context(nc.sbuf_tensor("work", [P, WORK // 4], F32))
        top = [0, 0]

        def carve(phase, nbytes, dt=F32):
            o = top[phase]
            top[phase] = o + nbytes
            assert top[phase] <= WORK, (phase, top[phase], WORK)
            v = work[:, o // 4:(o + nbytes) // 4]
            return v if dt == F32 else v.bitcast(dt)

        wT = carve(0, 4 * KT * D).rearrange("p (c n) -> p c n", c=KT)
        hT1 = [carve(0, 4 * D).rearrange("p (c t) -> p c t", c=KT) for _ in range(2)]
        xt = [carve(0, 4 * D) for _ in range(2)]
        xg = [carve(0, 4 * D) for _ in range(2)]
        x1 = [carve(0, 4 * D) for _ in range(2)]
        z1 = carve(0, 4 * D)
        z2 = carve(0, 4 * D)
        hf = carve(0, 4 * D)
        hs = [carve(0, 4 * D, F16).rearrange("p (s e) -> p s e", s=2) for _ in range(2)]
        ga = carve(0, 4 * D)
        gab = carve(0, 4 * D)
        NS = 3
        stg = [carve(0, 4 * D, I32) for _ in range(NS)]
        trn = [carve(0, 4 * D, I32) for _ in range(NS)]
        h2 = carve(1, 2 * 2 * H * NF, F16).rearrange("p (s c t) -> p s c t", s=2, c=NF)
        wd = carve(1, 2 * NF * D, F16).rearrange("p (c d) -> p c d", c=NF)
        hT_in = carve(1, 2 * 2 * D * BT, F16).rearrange("p (t e) -> p t e", t=BT)
        hT = hT_in.rearrange("p t (s c k) -> p s c t k", s=2, c=KT)
        io = [carve(1, 4 * H) for _ in range(4)]
        silu = carve(1, 4 * H)
        tmp = carve(1, 4 * H)
        top[1] -= 4 * 4 * H + 2 * 4 * H
        DC = A * CF * Q
        dstg = carve(1, 4 * D, I32)
        dtrn = carve(1, 4 * D, I32)
        pre = wgu[:, FT * 2 * D + D - 38912:].bitcast(F32)
        wst = [pre[:, 2048 * k:2048 * (k + 1)] for k in range(2)]
        mst = [pre[:, 4096 + 2048 * k:4096 + 2048 * (k + 1)].bitcast(I32) for k in range(2)]
        NM = 2
        PIECE = KT * H
        mp = [pre[:, 8192 + PIECE * k:8192 + PIECE * (k + 1)] for k in range(NM)]
        acc = pre[:, 16384:16384 + D].rearrange("p (h n) -> p h n", h=2)
        ones = pre[:, 17408:17408 + P]
        blk1 = pre[:, 17536:17536 + P]
        ident = carve(0, 4 * P)

        used = [0]

        def cols(n):
            used[0] += n
            assert used[0] <= 240
            return small[:, used[0] - n:used[0]]

        cvec = cols(KT)
        csil = cols(KT)
        colm = cols(4 * KT)
        sgs = cols(NF)
        sus = cols(NF)
        msum = cols(QB * KT)
        bnst = [cols(12) for _ in range(2)]
        mv = [cols(2) for _ in range(2)]
        ve = [cols(1) for _ in range(2)]
        rstd = [cols(1) for _ in range(2)]
        mhalf = cols(1)
        eps = cols(1)
        bmx = cols(4)
        bma = cols(4)
        sc = cols(10)
        spare = cols(5)

        pA = ctx.enter_context(nc.psum_tensor("pA", [P, 4, H], F32))
        pB = ctx.enter_context(nc.psum_tensor("pB", [P, 4, H], F32))
        z1T, z2T = pB[:, 0:2, :], pB[:, 2:4, :]
        colp = pB[:, 2, 0:4 * KT]
        sump = pB[:, 3, 0:QB * KT]
        rowp = pA[:, 2:4, :]

        def column_parts(v):
            dst = colm.rearrange("p (v u w) -> p v u w", v=4, u=2)
            src = colp.rearrange("p (v a u) -> p v a u", v=4, a=A)
            for a in range(A):
                for w in range(A):
                    yield dst[Q * a:Q * (a + 1), v:v + 2, :, w], src[Q * w:Q * (w + 1), v:v + 2, a, :]

        consts_set = sem("consts_set")
        c_loaded = sem("c_loaded")
        silu_c_done = sem("silu_c_done")
        scales_loaded = sem("scales_loaded")
        bias_loaded = sem("bias_loaded")
        ds_loaded = sem("ds_loaded")
        piece_loaded = [sem(f"piece_loaded{k}") for k in range(NM)]
        cols_used = sem("cols_used")
        rows_used = sem("rows_used")
        wm_loaded = [sem(f"wm_loaded{k}") for k in range(2)]
        mask_summed = sem("mask_summed")
        mask_total = sem("mask_total")
        mask_bits = sem("mask_bits")
        w_masked = sem("w_masked")
        w_turned = sem("w_turned")
        cols1_ready = sem("cols1_ready")
        cols2_ready = sem("cols2_ready")
        row_ready = sem("row_ready")
        ga_ready = sem("ga_ready")
        gb_ready = sem("gb_ready")
        bounds_in = sem("bounds_in")
        bounds_out = sem("bounds_out")
        dve_step = sem("dve_step")
        pool_step = sem("pool_step")
        x_loaded = [sem(f"x_loaded{k}") for k in range(2)]
        mv_done = [sem(f"mv_done{k}") for k in range(2)]
        ve_done = [sem(f"ve_done{k}") for k in range(2)]
        rstd_done = [sem(f"rstd_done{k}") for k in range(2)]
        z_done = [sem(f"z_done{k}") for k in range(2)]
        t_done = [sem(f"t_done{k}") for k in range(2)]
        hT1_ready = sem("hT1_ready")
        xg_ready = sem("xg_ready")
        attn_done = sem("attn_done")
        pair_free = sem("pair_free")
        x1_ready = sem("x1_ready")
        x1_stored = [sem(f"x1_stored{k}") for k in range(2)]
        hf_ready = sem("hf_ready")
        hi_ready = sem("hi_ready")
        lo_ready = sem("lo_ready")
        h_stored = [sem(f"h_stored{k}") for k in range(2)]
        unit_loaded = [sem(f"unit_loaded{k}") for k in range(NS)]
        unit_turned = sem("unit_turned")
        unit_cast = sem("unit_cast")
        dn_loaded = sem("dn_loaded")
        dn_turned = sem("dn_turned")
        dn_cast = sem("dn_cast")
        ht_loaded = sem("ht_loaded")
        gu_done = sem("gu_done")
        silu_done = sem("silu_done")
        h2_done = sem("h2_done")
        h2hi_done = sem("h2hi_done")
        down_done = sem("down_done")
        down_read = sem("down_read")
        tmp_ready = sem("tmp_ready")
        scaled = sem("scaled")
        res_ready = sem("res_ready")
        x1_loaded = [sem(f"x1_loaded{k}") for k in range(4)]
        res_stored = [sem(f"res_stored{k}") for k in range(4)]

        PIECE_COUNT = [16 * (m // NM + 1) for m in range(12)]
        UNIT_INC = 16 * A
        ND = FC * (D // P) + 1
        primed = (h2_done, res_ready, dn_turned, dn_cast, down_read)
        PRIMED = 1
        NCONST = 11
        block = ctx.enter_context(nc.Block())

        class Tile:
            def __init__(self, j, o):
                self.j, self.o = j, o
                self.n, self.half, self.par = 2 * j + o, j + o // 2, o % 2

            def __add__(self, d):
                return Tile(self.j, self.o + d)

        LAST = NT - 1
        FIRST_LOOPED, PAIRS = 3, (NT - 6) // 2

        def each_tile(eng, step):
            for i in range(FIRST_LOOPED):
                step(Tile(0, i))
            with eng.Fori(0, PAIRS) as j:
                step(Tile(j, FIRST_LOOPED))
                step(Tile(j, FIRST_LOOPED + 1))
            for i in range(FIRST_LOOPED + 2 * PAIRS, NT + 1):
                step(Tile(0, i))

        def units(t):
            if not isinstance(t.n, int) or 1 <= t.n <= NT - 2:
                for s in range(NS):
                    r = NS * (t.o - 1) + s
                    yield s, 2 * NS * t.j + r, NS * t.j + r // 2, r % 2
            elif t.n == LAST:
                yield 0, NS * (NT - 2), FT, 0
        NU = 2 * FT + 1
        assert NS * (NT - 2) == 2 * FT

        def static(t, lo, hi):
            return not isinstance(t.n, int) or lo <= t.n <= hi

        @block.sync
        def _(sp):
            def load_x(t):
                sp.dma_start(xt[t.par], x_v[t.n]).then_inc(x_loaded[t.par], 16)

            def load_piece(m):
                dst = mp[m % NM].rearrange("p (t n) -> p t n", t=KT)
                v, h = m // 2, m % 2
                sp.dma_start(dst, mod_v[:, :, v * D + h * H:v * D + (h + 1) * H]).then_inc(piece_loaded[m % NM], 16)

            def load_units(t):
                for s, u, c, g in units(t):
                    if static(t, 2, NT):
                        sp.wait_ge(unit_turned, u - NS + 1)
                    dst = stg[s].rearrange("p (b k) -> p b k", b=A)
                    for a in range(A):
                        rows = slice(Q * a, Q * (a + 1))
                        if isinstance(c, int) and c == FT:
                            for gg in range(2):
                                sp.dma_start(dst[rows, 2 * gg:2 * gg + 2], gu_l[gg][a]).then_inc(unit_loaded[s], 16)
                        else:
                            sp.dma_start(dst[rows], gu_v[g][c, a]).then_inc(unit_loaded[s], 16)

            load_x(Tile(0, 0))
            load_x(Tile(0, 1))
            for m in range(4):
                if m >= NM:
                    sp.wait_ge(cols_used, m - NM + 1)
                load_piece(m)
            for q in range(NQ):
                if q >= 2:
                    sp.wait_ge(w_turned, q - 1)
                for a in range(A):
                    rows = slice(Q * a, Q * (a + 1))
                    sp.dma_start(mst[q % 2].rearrange("p (b k) -> p b k", b=QB)[rows], m_v[q, a])\
                      .then_inc(wm_loaded[q % 2], 16)
                    sp.dma_start(wst[q % 2].rearrange("p (b k) -> p b k", b=QB)[rows], w_v[q, a])\
                      .then_inc(wm_loaded[q % 2], 16)
            for m in range(4, 12):
                if m < 6:
                    sp.wait_ge(cols_used, m - 1)
                elif m < 8:
                    sp.wait_ge(rows_used, m - 5)
                else:
                    sp.wait_ge(cols_used, m - 3)
                load_piece(m)

            def step(t):
                if static(t, 0, LAST - 3):
                    sp.wait_ge(z_done[0], t.n + 2)
                    sp.wait_ge(xg_ready, t.n + 2)
                    load_x(t + 3)
                load_units(t + 1)

            sp.wait_ge(z_done[0], 1)
            sp.wait_ge(xg_ready, 1)
            load_x(Tile(0, 2))
            each_tile(sp, step)

            def load_h(b):
                sp.dma_start(hT_in, h_blk[b].rearrange("p t e -> p t e")).then_inc(ht_loaded, 16)

            sp.wait_ge(unit_turned, NU)
            sp.wait_ge(xg_ready, NT)
            for k in range(2):
                sp.wait_ge(h_stored[k], 16 * (BT // 2))
            load_h(0)
            sp.wait_ge(unit_cast, NU)

            def load_dn(v, dq, fq):
                sp.wait_ge(dn_turned, v + PRIMED)
                for a in range(A):
                    dst = dstg[Q * a:Q * (a + 1), 0:DC].rearrange("p (b k) -> p b k", b=A)
                    sp.dma_start(dst, dn_v[dq, fq, a]).then_inc(dn_loaded, 16)

            with sp.Fori(0, D // P) as dq:
                for fq in range(FC):
                    load_dn(FC * dq + fq, dq, fq)
            sp.wait_ge(dn_turned, ND - 1 + PRIMED)
            for a in range(A):
                dst = dstg[Q * a:Q * (a + 1), :].rearrange("p (b k) -> p b k", k=Q)
                sp.dma_start(dst, dn_l[a % 2]).then_inc(dn_loaded, 16)
            sp.wait_ge(dn_cast, ND + PRIMED)

            G = 2 * BT
            def load_x1(b, g):
                if not isinstance(b, int) or b or g >= 4:
                    sp.wait_ge(res_stored[g % 4], 32 * b + 16 * (g // 4))
                sp.dma_start(io[g % 4], x1_d[BT * b + g // 2, :, (g % 2) * H:(g % 2 + 1) * H])\
                  .then_inc(x1_loaded[g % 4], 16)

            def store_block(b, last):
                for k in range(2):
                    sp.wait_ge(x1_stored[k], 16 * NT // 2)
                for g in range(4):
                    load_x1(b, g)
                if not last:
                    sp.wait_ge(gu_done, NF * b + NF)
                    for k in range(2):
                        sp.wait_ge(h_stored[k], 16 * NT // 2)
                    load_h(b + 1)
                for g in range(G):
                    sp.wait_ge(res_ready, G * b + g + 1 + PRIMED)
                    sp.dma_start(out_v[BT * b + g // 2, :, (g % 2) * H:(g % 2 + 1) * H], io[g % 4])\
                      .then_inc(res_stored[g % 4], 16)
                    if g < 4:
                        load_x1(b, g + 4)
            store_block(0, False)
            with sp.Fori(1, NB - 1) as b:
                store_block(b, False)
            store_block(NB - 1, True)
            for k in range(4):
                sp.wait_ge(res_stored[k], 16 * (2 * NT // 4))

        @block.gpsimd
        def _(pool):
            pool.memset(small[:, :], 0.0).then_inc(consts_set, 1)
            pool.memset(ident, 0.0).then_inc(consts_set, 1)
            pool.memset(ones, 1.0).then_inc(consts_set, 1)
            pool.memset(blk1, 0.0).then_inc(consts_set, 1)
            pool.wait_ge(consts_set, 4)
            pool.affine_select(out=ident, in_=ident, compare_op=ALU.not_equal, fill=1.0, base=0,
                               pattern=[[-1, P]], channel_multiplier=1).then_inc(consts_set, 1)
            for a in range(A):
                r = slice(Q * a, Q * (a + 1))
                pool.wait_ge(consts_set, 5 + a)
                pool.memset(blk1[r, r], 1.0).then_inc(consts_set, 1)
            pool.wait_ge(consts_set, 9)
            pool.memset(mhalf, -0.5).then_inc(consts_set, 1)
            pool.memset(eps, EPS).then_inc(consts_set, 1)
            pool.wait_ge(consts_set, NCONST)
            for k, s in enumerate(primed):
                pool.memset(spare[:, k:k + 1], 0.0).then_inc(s, PRIMED)

            def rstd_of(L, n):
                pool.wait_ge(mv_done[L], n + 1)
                pool.tensor_tensor(ve[L], mv[L][:, 1:2], eps, ALU.add).then_inc(ve_done[L], 1)
                pool.wait_ge(ve_done[L], n + 1)
                pool.tensor_tensor(rstd[L], ve[L], mhalf, ALU.pow).then_inc(rstd_done[L], 1)

            def add_bias(t):
                pool.wait_ge(x_loaded[t.par], 16 * t.half + 16)
                pool.tensor_tensor(xg[t.par], xt[t.par], gab, ALU.add).then_inc(xg_ready, 1)

            rstd_of(0, 0)
            rstd_of(0, 1)
            for q in range(NQ):
                pool.wait_ge(mask_bits, q + 1)
                w = wst[q % 2].rearrange("p (b i) -> p b i", i=Q)
                bits = msum.rearrange("p (b o) -> p b o", o=1).to_broadcast([P, QB * KT, Q])
                pool.tensor_tensor(w, w, bits, ALU.mult).then_inc(w_masked, 1)
            pool.wait_ge(ga_ready, 1)
            add_bias(Tile(0, 0))
            add_bias(Tile(0, 1))

            def step(t):
                if static(t, 0, LAST - 2):
                    rstd_of(0, t.n + 2)
                if static(t, 0, LAST):
                    rstd_of(1, t.n)
                    pool.wait_ge(x1_ready, t.n + 1)
                if static(t, 0, LAST - 2):
                    add_bias(t + 2)
                if static(t, 0, LAST):
                    pool.dma_start(x1_d[t.n], x1[t.par]).then_inc(x1_stored[t.par], 16)
                if isinstance(t.n, int) and t.n == 0:
                    pool.wait_ge(bounds_in, 4)
                    pool.partition_all_reduce(bma, bmx, P, bass.bass_isa.ReduceOp.max).then_inc(bounds_out, 1)
                if static(t, 1, NT):
                    r = t + (-1)
                    pool.wait_ge(hi_ready, r.n + 1)
                    pool.tensor_tensor(hs[r.par][:, 1, :], hf, hs[r.par][:, 0, :], ALU.subtract).then_inc(lo_ready, 1)
                    pool.wait_ge(lo_ready, r.n + 1)
                    pool.dma_start(h_d[r.n], hs[r.par].rearrange("p s e -> p (s e)")).then_inc(h_stored[r.par], 16)

            each_tile(pool, step)

            def finish(q, k, loaded):
                pool.wait_ge(down_read, q + 1 + PRIMED)
                pool.tensor_tensor(tmp, tmp, gbs[:, (k % 2) * H:(k % 2 + 1) * H], ALU.mult).then_inc(scaled, 1)
                pool.wait_ge(scaled, q + 1)
                pool.wait_ge(x1_loaded[k], loaded)
                pool.tensor_tensor(io[k], tmp, io[k], ALU.add).then_inc(res_ready, 1)

            with pool.Fori(0, 2 * NB) as r:
                for k in range(4):
                    finish(4 * r + k, k, 16 * r + 16)

        @block.scalar
        def _(act):
            act.wait_ge(consts_set, NCONST)
            act.dma_start(cvec, c_in.rearrange("o (p t) -> (o p) t", p=P)).then_inc(c_loaded, 16)
            act.dma_start(gab, bias.rearrange("(o n) -> o n", o=1).to_broadcast([P, D])).then_inc(bias_loaded, 16)
            act.dma_start(gbs[:, :], down_s.rearrange("n o -> o n").to_broadcast([P, D])).then_inc(ds_loaded, 16)
            for s_in, s_col, r in ((gate_s, sgs, 0), (up_s, sus, P // 2)):
                for a in range(A):
                    src = s_in[FA * a:FA * (a + 1), :].rearrange("(c i) o -> i (c o)", i=Q)
                    act.dma_start(s_col[Q * a:Q * (a + 1), 0:FT], src).then_inc(scales_loaded, 16)
                act.dma_start(s_col[r:r + FL, FT:NF], s_in[FT * P:F, :]).then_inc(scales_loaded, 16)
            act.wait_ge(c_loaded, 16)
            act.activation(csil, cvec, ACT.Silu).then_inc(silu_c_done, 1)
            act.wait_ge(cols_used, 4)
            for dst, src in column_parts(0):
                last = act.activation(dst, src, ACT.Copy)
            last.then_inc(cols1_ready, 1)
            act.wait_ge(cols1_ready, 1)
            act.activation(colm[:, KT:2 * KT], colm[:, KT:2 * KT], ACT.Copy, bias=1.0).then_inc(cols1_ready, 1)
            act.wait_ge(cols1_ready, 2)

            def shift_scale(dst, src, L):
                for c in range(KT):
                    last = act.activation(dst[:, c, :], src[:, c, :], ACT.Identity,
                                          scale=colm[:, (2 * L + 1) * KT + c:(2 * L + 1) * KT + c + 1],
                                          bias=colm[:, 2 * L * KT + c:2 * L * KT + c + 1])
                return last

            z1T_c = z1T.rearrange("p h (c t) -> p (h c) t", t=P)
            z2T_c = z2T.rearrange("p h (c t) -> p (h c) t", t=P)
            hf_c = hf.rearrange("p (c t) -> p c t", c=KT)

            def turn_out(t):
                act.wait_ge(t_done[0], t.n + 1)
                if static(t, 2, NT):
                    act.wait_ge(attn_done, t.n - 1)
                shift_scale(hT1[t.par], z1T_c, 0).then_inc(hT1_ready, 1)

            turn_out(Tile(0, 0))

            def step(t):
                if static(t, 0, LAST - 1):
                    turn_out(t + 1)
                if isinstance(t.n, int) and t.n == 1:
                    act.wait_ge(cols2_ready, 2)
                    act.wait_ge(gb_ready, 1)
                    act.wait_ge(w_turned, NQ)
                for s, u, c, g in units(t):
                    act.wait_ge(unit_turned, u + 1)
                    act.activation(wgu_u[:, 2 * c + g, :], trn[s], ACT.Copy).then_inc(unit_cast, 1)
                if static(t, 1, NT):
                    r = t + (-1)
                    act.wait_ge(t_done[1], r.n + 1)
                    if static(r, 1, NT):
                        act.wait_ge(lo_ready, r.n)
                    shift_scale(hf_c, z2T_c, 1).then_inc(hf_ready, 1)
                    act.wait_ge(hf_ready, r.n + 1)
                    if static(r, 2, NT):
                        act.wait_ge(h_stored[r.par], 16 * r.half)
                    act.activation(hs[r.par][:, 0, :], hf, ACT.Copy).then_inc(hi_ready, 1)

            each_tile(act, step)

            def tile_out(n, c, k):
                act.wait_ge(gu_done, n + 1)
                act.wait_ge(h2_done, n + PRIMED)
                act.activation(silu, pA[:, 2 * k, :], ACT.Silu, scale=sgs[:, bass.ds(c, 1)]).then_inc(silu_done, 1)
                act.wait_ge(h2_done, n + 1 + PRIMED)
                act.activation(h2[:, 0, c, :], pA[:, 2 * k + 1, :], ACT.Copy, scale=1.0 / LO).then_inc(h2hi_done, 1)

            def last_tile_out(n):
                k, lo_h, up_h = 2 * ((NF - 1) % 2), slice(0, FL), slice(FL, P)
                act.wait_ge(gu_done, n + 1)
                act.wait_ge(h2_done, n + PRIMED)
                act.activation(silu[up_h], pA[lo_h, k, :], ACT.Silu, scale=sgs[lo_h, FT:NF]).then_inc(silu_done, 1)
                act.wait_ge(h2_done, n + 1 + PRIMED)
                act.activation(h2[lo_h, 0, FT, :], pA[up_h, k, :], ACT.Copy, scale=1.0 / LO)
                act.activation(h2[up_h, 0, FT, :], pA[up_h, k, :], ACT.Copy, scale=1.0 / LO).then_inc(h2hi_done, 1)

            def dn_out(v, dq, fq):
                act.wait_ge(dn_turned, v + 1 + PRIMED)
                dst = wd[:, CF * fq:CF * (fq + 1), bass.ds(P * dq, P)]
                act.activation(dst, dtrn[:, 0:DC].rearrange("p (c d) -> p c d", c=CF), ACT.Copy).then_inc(dn_cast, 1)

            def last_dn_out():
                act.wait_ge(dn_turned, ND + PRIMED)
                act.activation(wd[0:FL, FT, :], dtrn[0:FL, :], ACT.Copy)
                act.activation(wd[FL:P, FT, :], dtrn[FL:P, :], ACT.Copy, scale=1.0 / LO).then_inc(dn_cast, 1)

            def out_half(q, k):
                act.wait_ge(down_done, q + 1)
                act.wait_ge(res_ready, q + PRIMED)
                act.activation(tmp, pB[:, 2 * k, :], ACT.Copy).then_inc(tmp_ready, 1)

            def down_out(b):
                with act.Fori(0, BT) as ts:
                    for k in range(2):
                        out_half(2 * BT * b + 2 * ts + k, k)

            for k in range(2):
                act.wait_ge(x1_stored[k], 16 * NT // 2)
                act.wait_ge(h_stored[k], 16 * NT // 2)
            with act.Fori(0, D // P) as j:
                for k in range(2):
                    tile_out(2 * j + k, 2 * j + k, k)
                for fq in range(FC):
                    dn_out(FC * j + fq, j, fq)
            with act.Fori(D // P, FT // 2) as j:
                for k in range(2):
                    tile_out(2 * j + k, 2 * j + k, k)
            tile_out(FT - 1, FT - 1, 0)
            last_dn_out()
            last_tile_out(FT)
            down_out(0)
            with act.Fori(1, NB) as b:
                with act.Fori(0, FT // 2) as j:
                    for k in range(2):
                        tile_out(NF * b + 2 * j + k, 2 * j + k, k)
                tile_out(NF * b + FT - 1, FT - 1, 0)
                last_tile_out(NF * b + FT)
                down_out(b)

        @block.tensor
        def _(pe):
            def transpose(L, t):
                z, dst, taken = ((z1, z1T, hT1_ready), (z2, z2T, hf_ready))[L]
                zc = z.rearrange("p (c k) -> p c k", c=KT)
                pe.wait_ge(z_done[L], t.n + 1)
                if static(t, 1, NT):
                    pe.wait_ge(taken, t.n)
                for c in range(KT):
                    last = pe.transpose(dst[:, c // 4, (c % 4) * P:(c % 4 + 1) * P], zc[:, c], ident)
                last.then_inc(t_done[L], 1)

            def attend(t):
                pe.wait_ge(hT1_ready, t.n + 1)
                if static(t, 2, NT):
                    pe.wait_ge(pair_free, t.n - 1)
                for h in range(2):
                    for c in range(KT):
                        last = pe.matmul(pA[:, 2 * t.par + h, :], hT1[t.par][:, c, :], wT[:, c, h * H:(h + 1) * H],
                                         start=(c == 0), stop=(c == KT - 1))
                last.then_inc(attn_done, 1)

            def column_piece(m, v, h):
                pe.wait_ge(piece_loaded[m % NM], PIECE_COUNT[m])
                w = mp[m % NM].rearrange("p (t c k) -> p t c k", t=KT, c=KT // 2)
                for c in range(KT // 2):
                    col = KT * v + h * (KT // 2) + c
                    for t in range(KT):
                        last = pe.matmul(colp[:, col:col + 1], w[:, t, c], csil[:, t:t + 1],
                                         start=(t == 0), stop=(t == KT - 1))
                last.then_inc(cols_used, 1)

            def gate_row(g):
                for h in range(2):
                    last = pe.matmul(rowp[:, h, :], ones, acc[:, h, :], start=True, stop=True)
                last.then_inc(row_ready, 1)

            pe.wait_ge(consts_set, NCONST)
            transpose(0, Tile(0, 0))
            pe.wait_ge(silu_c_done, 1)
            for m in range(4):
                column_piece(m, m // 2, m % 2)
            for q in range(NQ):
                pe.wait_ge(mask_summed, q + 1)
                pe.matmul(sump, blk1, msum, start=True, stop=True).then_inc(mask_total, 1)

            def step(t):
                if static(t, 0, LAST - 1):
                    transpose(0, t + 1)
                if isinstance(t.n, int) and t.n == 0:
                    pe.wait_ge(w_turned, NQ)
                if isinstance(t.n, int) and t.n == 1:
                    pe.wait_ge(gb_ready, 1)
                    pe.wait_ge(cols2_ready, 2)
                if static(t, 0, LAST):
                    attend(t)
                if isinstance(t.n, int) and t.n == 0:
                    pe.wait_ge(rows_used, 2)
                    gate_row(0)
                    for m in range(6, 10):
                        column_piece(m, m // 2 - 1, m % 2)
                    pe.wait_ge(rows_used, 4)
                    pe.wait_ge(ga_ready, 1)
                    gate_row(1)
                if static(t, 1, NT):
                    transpose(1, t + (-1))

            each_tile(pe, step)

            def gate_up(b, n, c, k):
                pe.wait_ge(ht_loaded, 16 * b + 16)
                pe.wait_ge(pair_free, NT + n - 1)
                for g in range(2):
                    for kc in range(KT):
                        for s in range(2):
                            last = pe.matmul(pA[:, 2 * k + g, :], wgu_u[:, 2 * c + g, P * kc:P * (kc + 1)], hT[:, s, kc],
                                             start=(kc == 0 and s == 0), stop=(kc == KT - 1 and s == 1))
                last.then_inc(gu_done, 1)

            def last_gate_up(n):
                pe.wait_ge(pair_free, NT + n - 1)
                for kc in range(KT):
                    for s in range(2):
                        last = pe.matmul(pA[:, 2 * ((NF - 1) % 2), :], wgu_u[:, 2 * FT, P * kc:P * (kc + 1)], hT[:, s, kc],
                                         start=(kc == 0 and s == 0), stop=(kc == KT - 1 and s == 1))
                last.then_inc(gu_done, 1)

            def down(b, ts, k):
                q = 2 * BT * b + 2 * ts + k
                pe.wait_ge(pair_free, NT + NF * b + FT)
                for c in range(FT):
                    for s in range(2):
                        pe.matmul(pB[:, 2 * k + s, :], h2[:, s, c, bass.ds(P * ts, P)], wd[:, c, k * H:(k + 1) * H],
                                  start=(c == 0), stop=(c == FT - 1 and s == 1))
                pe.wait_ge(pair_free, NT + NF * b + NF)
                pe.matmul(pB[:, 2 * k, :], h2[:, 0, FT, bass.ds(P * ts, P)], wd[:, FT, k * H:(k + 1) * H],
                          start=False, stop=True).then_inc(down_done, 1)
                pe.wait_ge(down_read, q + PRIMED)

            with pe.Fori(0, NB) as b:
                pe.wait_ge(unit_cast, NU)
                with pe.Fori(0, FT // 2) as j:
                    for k in range(2):
                        gate_up(b, NF * b + 2 * j + k, 2 * j + k, k)
                gate_up(b, NF * b + FT - 1, FT - 1, 0)
                last_gate_up(NF * b + FT)
                pe.wait_ge(hf_ready, NT)
                pe.wait_ge(dn_cast, ND + PRIMED)
                with pe.Fori(0, BT) as ts:
                    for k in range(2):
                        down(b, ts, k)

        @block.vector
        def _(dve):
            steps = [0]

            def link(ins):
                steps[0] += 1
                ins.then_inc(dve_step, 1)
                dve.wait_ge(dve_step, steps[0])

            def stats(L, n, src):
                for h in range(2):
                    dve.bn_stats(bnst[L][:, 6 * h:6 * h + 6], src[:, h * H:(h + 1) * H])
                dve.drain()
                dve.bn_aggr(mv[L], bnst[L]).then_inc(mv_done[L], 1)

            def normalise(L, n, src, first):
                z = (z1, z2)[L]
                dve.wait_ge(rstd_done[L], n + 1)
                if not first:
                    dve.wait_ge(t_done[L], n)
                dve.tensor_scalar(z.rearrange("p (c a i) -> p a c i", c=KT, a=A),
                                  src.rearrange("p (a c i) -> p a c i", c=KT, a=A),
                                  mv[L][:, 0:1], rstd[L], ALU.subtract, ALU.mult).then_inc(z_done[L], 1)

            def norm1(t):
                dve.wait_ge(x_loaded[t.par], 16 * t.half + 16)
                stats(0, t.n, xt[t.par])
                normalise(0, t.n, xt[t.par], not static(t, 1, NT))

            def after_attention(t):
                dve.wait_ge(attn_done, t.n + 1)
                if static(t, 2, NT):
                    dve.wait_ge(x1_stored[t.par], 16 * t.half)
                ps = pA[:, 2 * t.par:2 * t.par + 2, :].rearrange("p h n -> p (h n)")
                dve.tensor_tensor(x1[t.par], ps, ga, ALU.mult).then_inc(pair_free, 1)
                dve.wait_ge(pair_free, t.n + 1)
                dve.wait_ge(xg_ready, t.n + 1)
                dve.tensor_tensor(x1[t.par], x1[t.par], xg[t.par], ALU.add).then_inc(x1_ready, 1)
                dve.wait_ge(x1_ready, t.n + 1)
                stats(1, t.n, x1[t.par])
                normalise(1, t.n, x1[t.par], not static(t, 1, NT))

            def turn_units(t):
                for s, u, c, g in units(t):
                    dve.wait_ge(unit_loaded[s], UNIT_INC * t.n if not (isinstance(c, int) and c == FT)
                                else UNIT_INC * (NT - 2) + 2 * UNIT_INC)
                    if static(t, 2, NT):
                        dve.wait_ge(unit_cast, u - NS + 1)
                    dve.transpose(trn[s].rearrange("p (c b i) -> p c b i", c=KT, b=A),
                                  stg[s].rearrange("p (b c i) -> p c b i", b=A, c=KT)).then_inc(unit_turned, 1)

            def sum_row(m, h):
                dve.wait_ge(piece_loaded[m % NM], PIECE_COUNT[m])
                w = mp[m % NM].rearrange("p (t n) -> p t n", t=KT)
                link(dve.tensor_scalar(acc[:, h], w[:, 0], csil[:, 0:1], None, ALU.mult))
                for t in range(1, KT):
                    last = dve.scalar_tensor_tensor(out=acc[:, h], in0=w[:, t], scalar=csil[:, t:t + 1], in1=acc[:, h],
                                                    op0=ALU.mult, op1=ALU.add)
                    if t < KT - 1:
                        link(last)
                last.then_inc(rows_used, 1)

            def clamp_gate(dst, tmp_row, src):
                link(dve.tensor_scalar(tmp_row, src, 0.0, 2.0, ALU.is_ge, ALU.mult))
                link(dve.tensor_scalar(dst, src, -1.0, GATE_FLOOR, ALU.mult, ALU.max))
                link(dve.tensor_tensor(dst, src, dst, ALU.max))
                link(dve.scalar_tensor_tensor(out=dst, in0=tmp_row, scalar=-1.0, in1=dst, op0=ALU.add, op1=ALU.mult))

            dve.wait_ge(consts_set, NCONST)
            norm1(Tile(0, 0))
            dve.wait_ge(x_loaded[1], 16)
            stats(0, 1, xt[1])
            normalise(0, 1, xt[1], False)
            for q in range(NQ):
                dve.wait_ge(wm_loaded[q % 2], 2 * A * 16 * (q // 2 + 1))
                if q:
                    dve.wait_ge(w_masked, q)
                dve.tensor_reduce(msum, mst[q % 2].rearrange("p (b i) -> p b i", i=Q), AXX, ALU.add)\
                   .then_inc(mask_summed, 1)
                dve.wait_ge(mask_total, q + 1)
                dve.tensor_scalar(msum, sump, 0.0, None, ALU.is_gt).then_inc(mask_bits, 1)
                dve.wait_ge(w_masked, q + 1)
                dve.transpose(wT[:, :, QB * Q * q:QB * Q * (q + 1)].rearrange("p c (b i) -> p c b i", i=Q),
                              wst[q % 2].rearrange("p (b c i) -> p c b i", b=QB, c=KT)).then_inc(w_turned, 1)
            dve.wait_ge(silu_c_done, 1)
            for h in range(2):
                sum_row(4 + h, h)
            dve.wait_ge(row_ready, 1)
            rowf = rowp.rearrange("p h n -> p (h n)")
            clamp_gate(ga, x1[1], rowf)
            dve.wait_ge(bias_loaded, 16)
            dve.tensor_tensor(gab, gab, ga, ALU.mult).then_inc(ga_ready, 1)
            dve.wait_ge(ga_ready, 1)

            def scales():
                dve.wait_ge(cols_used, 8)
                dve.wait_ge(scales_loaded, 16 * 2 * (A + 1))
                s_b, one_cb = colm[:, 2 * KT:3 * KT], colm[:, 3 * KT:4 * KT]
                for dst, src in column_parts(2):
                    last = dve.tensor_copy(dst, src)
                link(last)
                link(dve.tensor_scalar(one_cb, one_cb, 1.0, None, ALU.add))
                for k, v in enumerate((one_cb, s_b, sgs, sus)):
                    mag = msum[:, 0:v.shape[1]]
                    link(dve.scalar_tensor_tensor(out=mag, in0=v, scalar=-1.0, in1=v, op0=ALU.mult, op1=ALU.max))
                    dve.tensor_reduce(bmx[:, k:k + 1], mag, AXX, ALU.max).then_inc(bounds_in, 1)
                    dve.wait_ge(bounds_in, k + 1)
                dve.wait_ge(bounds_out, 1)
                b1, g1, p1, s1, i1, b2, u2, p2, s2, i2 = (sc[:, k:k + 1] for k in range(10))

                def power(bound, p, s, inv):
                    link(dve.tensor_scalar(bound, bound, 2.0 ** -60, 2.0 ** 60, ALU.max, ALU.min))
                    link(dve.tensor_scalar(p.bitcast(I32), bound.bitcast(I32), 0x7F800000, None, ALU.bitwise_and))
                    link(dve.tensor_scalar(s.bitcast(I32), p.bitcast(I32), -1.0, float((2 * 127 + 14) << 23),
                                           ALU.mult, ALU.add))
                    link(dve.tensor_scalar(inv, p, 2.0 ** -14, None, ALU.mult))

                link(dve.tensor_scalar(b1, bma[:, 0:1], bma[:, 1:2], float(D) ** 0.5, ALU.add, ALU.mult))
                link(dve.tensor_scalar(g1, b1, float(D) ** 0.5 * W_MAX, None, ALU.mult))
                power(b1, p1, s1, i1)
                link(dve.tensor_scalar(u2, g1, bma[:, 3:4], None, ALU.mult))
                link(dve.tensor_scalar(b2, g1, bma[:, 2:3], u2, ALU.mult, ALU.mult))
                power(b2, p2, s2, i2)
                link(dve.tensor_scalar(s2, s2, LO, None, ALU.mult))
                link(dve.tensor_scalar(sgs, sgs, i1, None, ALU.mult))
                link(dve.tensor_scalar(sus, sus, i1, s2, ALU.mult, ALU.mult))
                dve.tensor_scalar(one_cb, one_cb, s1, None, ALU.mult).then_inc(cols2_ready, 1)
                dve.tensor_scalar(s_b, s_b, s1, None, ALU.mult).then_inc(cols2_ready, 1)
                for h in range(2):
                    sum_row(10 + h, h)
                dve.wait_ge(row_ready, 2)
                dve.wait_ge(ds_loaded, 16)
                clamp_gate(hf, x1[1], rowf)
                link(dve.tensor_tensor(gbs[:, :], gbs[:, :], hf, ALU.mult))
                dve.tensor_scalar(gbs[:, :], gbs[:, :], i2, None, ALU.mult).then_inc(gb_ready, 1)

            def step(t):
                turn_units(t)
                if static(t, 0, LAST - 2):
                    norm1(t + 2)
                if static(t, 0, LAST):
                    after_attention(t)
                if isinstance(t.n, int) and t.n == 0:
                    scales()

            each_tile(dve, step)

            def tile_out(n, c, k):
                dve.wait_ge(silu_done, n + 1)
                up = pA[:, 2 * k + 1, :]
                dve.scalar_tensor_tensor(out=up, in0=up, scalar=sus[:, bass.ds(c, 1)], in1=silu, op0=ALU.mult, op1=ALU.mult)\
                   .then_inc(h2_done, 1)
                dve.wait_ge(h2_done, n + 1 + PRIMED)
                dve.wait_ge(h2hi_done, n + 1)
                dve.scalar_tensor_tensor(out=h2[:, 1, c, :], in0=h2[:, 0, c, :], scalar=-LO, in1=up,
                                         op0=ALU.mult, op1=ALU.add).then_inc(pair_free, 1)

            def last_tile_out(n):
                up_h = slice(FL, P)
                dve.wait_ge(silu_done, n + 1)
                up = pA[up_h, 2 * ((NF - 1) % 2), :]
                dve.scalar_tensor_tensor(out=up, in0=up, scalar=sus[up_h, FT:NF], in1=silu[up_h], op0=ALU.mult,
                                         op1=ALU.mult).then_inc(h2_done, 1)
                dve.wait_ge(h2_done, n + 1 + PRIMED)
                dve.wait_ge(h2hi_done, n + 1)
                dve.scalar_tensor_tensor(out=h2[up_h, 0, FT, :], in0=h2[up_h, 0, FT, :], scalar=-LO, in1=up,
                                         op0=ALU.mult, op1=ALU.add).then_inc(pair_free, 1)

            def turn_dn(v):
                dve.wait_ge(dn_loaded, A * 16 * (v + 1))
                dve.wait_ge(dn_cast, v + PRIMED)
                dve.transpose(dtrn[:, 0:DC].rearrange("p (c b i) -> p c b i", c=CF, b=A),
                              dstg[:, 0:DC].rearrange("p (b c i) -> p c b i", b=A, c=CF)).then_inc(dn_turned, 1)

            def down_out(b):
                with dve.Fori(0, BT) as ts:
                    for k in range(2):
                        dve.wait_ge(tmp_ready, 2 * BT * b + 2 * ts + k + 1)
                        dve.scalar_tensor_tensor(out=tmp, in0=pB[:, 2 * k + 1, :], scalar=1.0 / LO, in1=tmp,
                                                 op0=ALU.mult, op1=ALU.add).then_inc(down_read, 1)

            with dve.Fori(0, D // P) as j:
                for k in range(2):
                    tile_out(2 * j + k, 2 * j + k, k)
                for fq in range(FC):
                    turn_dn(FC * j + fq)
            with dve.Fori(D // P, FT // 2) as j:
                for k in range(2):
                    tile_out(2 * j + k, 2 * j + k, k)
            tile_out(FT - 1, FT - 1, 0)
            dve.wait_ge(dn_loaded, A * 16 * ND)
            dve.wait_ge(dn_cast, ND - 1 + PRIMED)
            dve.transpose(dtrn, dstg).then_inc(dn_turned, 1)
            last_tile_out(FT)
            down_out(0)
            with dve.Fori(1, NB) as b:
                with dve.Fori(0, FT // 2) as j:
                    for k in range(2):
                        tile_out(NF * b + 2 * j + k, 2 * j + k, k)
                tile_out(NF * b + FT - 1, FT - 1, 0)
                last_tile_out(NF * b + FT)
                down_out(b)


_INS = ['L0_attn_data', 'L0_attn_mask', 'L0_attn_weight', 'L0_attn_bias', 'L0_ffn_gate_w', 'L0_ffn_gate_s',
        'L0_ffn_up_w', 'L0_ffn_up_s', 'L0_ffn_down_w', 'L0_ffn_down_s', 'L0_c', 'L0_wmod']


def kernel(**inputs):
    import numpy as np
    import concourse.bacc as bacc
    from concourse.bass_utils import run_bass_kernel_spmd

    nc = bacc.Bacc("TRN2", target_bir_lowering=False, num_devices=1)
    arrays, args = {}, []
    for name in _INS:
        a = np.ascontiguousarray(inputs[name])
        arrays[f"in_{name}"] = a
        args.append(nc.dram_tensor(f"in_{name}", a.shape, mybir.dt.from_np(a.dtype), kind="ExternalInput").ap())
    shape = np.asarray(inputs['L0_attn_data']).shape
    out = nc.dram_tensor("out_0", shape, F32, kind="ExternalOutput").ap()
    adaln_kernel(nc, *args, out)
    r = run_bass_kernel_spmd(nc, [arrays], core_ids=[0])
    return r.results[0]["out_0"]
```

```python
from contextlib import ExitStack

import concourse.bass as bass
from concourse import mybir

F32 = mybir.dt.float32
F16 = mybir.dt.float16
I32 = mybir.dt.int32
ALU = mybir.AluOpType
ACT = mybir.ActivationFunctionType
AXX = mybir.AxisListType.X

P = 128
EPS = 1e-5
GATE_FLOOR = 0.25


def adaln_kernel(nc, data, mask, weight, bias, gate_w, gate_s, up_w, up_s, down_w, down_s, c_in, wmod, out):
    T, D = data.shape[1], data.shape[2]
    F = gate_w.shape[0]
    Q = 32
    A = P // Q
    KT = D // P
    KA = D // A
    NT = T // P
    H = 512
    FT = F // P
    FL = F - FT * P
    FA = FT * Q
    NF = FT + 1
    assert FL == P // 2 and NF % 2 == 0 and D == 2 * H and KA == KT * Q
    BT = H // P
    NB = T // H
    NQ = 4
    QB = D // Q // NQ
    FC = 3
    CF = FT // FC
    LO = 2048.0
    W_MAX = 128.0

    x_v = data.rearrange("o (n p) d -> (o n) p d", p=P)
    out_v = out.rearrange("o (n p) d -> (o n) p d", p=P)
    x1_d = nc.dram_tensor("x1_scratch", (NT, P, D), F32).ap()
    h_d = nc.dram_tensor("h_scratch", (NT, P, 2 * D), F16).ap()
    h_blk = h_d.rearrange("(b t) p e -> b p t e", t=BT)
    w_v = weight.rearrange("(q b j) (a k) -> q a j b k", q=NQ, j=Q, a=A)
    m_v = mask.rearrange("(q b j) (a k) -> q a j b k", q=NQ, j=Q, a=A)
    gu_v = [w[0:FT * P, :].rearrange("(b q j) (a k) -> q a j b k", b=A, j=Q, a=A) for w in (gate_w, up_w)]
    gu_l = [w[FT * P:F, :].rearrange("(b j) (a k) -> a j b k", j=Q, a=A) for w in (gate_w, up_w)]
    dn_v = down_w[:, 0:FT * P].rearrange("(d b j) (a g k) -> d g a j b k", b=A, j=Q, a=A, g=FC)
    dn_l = down_w[:, FT * P:F].rearrange("(b j) (a k) -> a j b k", j=Q, k=Q)
    mod_v = wmod.rearrange("(p t) n -> p t n", p=P)

    with ExitStack() as ctx:
        ctx.enter_context(nc.allow_non_contiguous_dma(reason="the scales of the weights, once, 22 KB"))
        def sem(name):
            return ctx.enter_context(nc.semaphore(name))

        wgu = ctx.enter_context(nc.sbuf_tensor("wgu", [P, FT * 2 * D + D], F16))
        wgu_u = wgu[:, :].rearrange("p (u e) -> p u e", e=D)
        gbs = ctx.enter_context(nc.sbuf_tensor("gbs", [P, D], F32))
        small = ctx.enter_context(nc.sbuf_tensor("small", [P, 208], F32))
        WORK = nc.sbuf_bytes_remaining // 64 * 64
        work = ctx.enter_context(nc.sbuf_tensor("work", [P, WORK // 4], F32))
        top = [0, 0]

        def carve(phase, nbytes, dt=F32):
            o = top[phase]
            top[phase] = o + nbytes
            assert top[phase] <= WORK, (phase, top[phase], WORK)
            v = work[:, o // 4:(o + nbytes) // 4]
            return v if dt == F32 else v.bitcast(dt)

        wT = carve(0, 4 * KT * D).rearrange("p (c n) -> p c n", c=KT)
        hT1 = [carve(0, 4 * D).rearrange("p (c t) -> p c t", c=KT) for _ in range(2)]
        xt = [carve(0, 4 * D) for _ in range(2)]
        xg = [carve(0, 4 * D) for _ in range(2)]
        x1 = [carve(0, 4 * D) for _ in range(2)]
        z1 = carve(0, 4 * D)
        z2 = carve(0, 4 * D)
        hf = carve(0, 4 * D)
        hs = [carve(0, 4 * D, F16).rearrange("p (s e) -> p s e", s=2) for _ in range(2)]
        ga = carve(0, 4 * D)
        gab = carve(0, 4 * D)
        NS = 3
        stg = [carve(0, 4 * D, I32) for _ in range(NS)]
        trn = [carve(0, 4 * D, I32) for _ in range(NS)]
        h2 = carve(1, 2 * 2 * H * NF, F16).rearrange("p (s c t) -> p s c t", s=2, c=NF)
        wd = carve(1, 2 * NF * D, F16).rearrange("p (c d) -> p c d", c=NF)
        hT_in = carve(1, 2 * 2 * D * BT, F16).rearrange("p (t e) -> p t e", t=BT)
        hT = hT_in.rearrange("p t (s c k) -> p s c t k", s=2, c=KT)
        io = [carve(1, 4 * H) for _ in range(4)]
        silu = carve(1, 4 * H)
        tmp = carve(1, 4 * H)
        top[1] -= 4 * 4 * H + 2 * 4 * H
        DC = A * CF * Q
        dstg = carve(1, 4 * D, I32)
        dtrn = carve(1, 4 * D, I32)
        pre = wgu[:, :].bitcast(F32)
        wst = [pre[:, 2048 * k:2048 * (k + 1)] for k in range(2)]
        mst = [pre[:, 4096 + 2048 * k:4096 + 2048 * (k + 1)].bitcast(I32) for k in range(2)]
        NM = 3
        PIECE = KT * H
        mp = [pre[:, 8192 + PIECE * k:8192 + PIECE * (k + 1)] for k in range(NM)]
        mp.append(pre[:, 8192 - PIECE:8192])
        mp += [work[:, (NF * s + 4) * H // 2:(NF * s + 4) * H // 2 + PIECE] for s in range(2)]
        o = 8192 + NM * PIECE
        acc_a = pre[:, o:o + D]
        blk1 = pre[:, o + D:o + D + P]
        o += D + P
        msum = [pre[:, o + QB * KT * q:o + QB * KT * (q + 1)] for q in range(NQ)]
        acc = [acc_a, hf, acc_a, hf, acc_a, gbs[:, :]]
        ds = z1
        sgn = xt[1]
        ident = carve(0, 4 * P)

        used = [0]

        def cols(n):
            used[0] += n
            assert used[0] <= 208
            return small[:, used[0] - n:used[0]]

        cvec = cols(KT)
        csil = cols(KT)
        colm = cols(4 * KT)
        sgs = cols(NF)
        sus = cols(NF)
        mag = cols(NF)
        bnst = [cols(12) for _ in range(2)]
        mv = [cols(2) for _ in range(2)]
        ve = [cols(1) for _ in range(2)]
        rstd = [cols(1) for _ in range(2)]
        mhalf = cols(1)
        eps = cols(1)
        one = cols(1)
        two = cols(1)
        bmx = cols(4)
        bma = cols(4)
        sc = cols(10)
        spare = cols(5)

        pA = ctx.enter_context(nc.psum_tensor("pA", [P, 4, H], F32))
        pB = ctx.enter_context(nc.psum_tensor("pB", [P, 4, H], F32))
        z1T, z2T = pB[:, 0:2, :], pB[:, 2:4, :]
        colp = pB[:, 2, 0:2 * KT]
        colp2 = pA[:, 1, 0:2 * KT]
        sump = [bank[:, 0:QB * KT] for bank in (pA[:, 2], pA[:, 3], pA[:, 1], pB[:, 3])]
        rowp = [pB[:, 2:4, :].rearrange("p h n -> p (h n)"),
                pB[:, 0:2, :].rearrange("p h n -> p (h n)")]

        consts_set = sem("consts_set")
        c_loaded = sem("c_loaded")
        silu_c_done = sem("silu_c_done")
        scales_loaded = sem("scales_loaded")
        bias_loaded = sem("bias_loaded")
        ds_loaded = sem("ds_loaded")
        piece_loaded = [sem(f"piece_loaded{k}") for k in range(NM + 3)]
        dve_summed = sem("dve_summed")
        pool_summed = sem("pool_summed")
        piece_scaled = sem("piece_scaled")
        acc_used = sem("acc_used")
        cols2_copied = sem("cols2_copied")
        m_loaded = [sem(f"m_loaded{k}") for k in range(2)]
        w_loaded = [sem(f"w_loaded{k}") for k in range(2)]
        mask_summed = sem("mask_summed")
        mask_total = sem("mask_total")
        mask_bits = sem("mask_bits")
        w_masked = [sem(f"w_masked{k}") for k in range(2)]
        w_turned = [sem(f"w_turned{k}") for k in range(2)]
        cols1_ready = sem("cols1_ready")
        cols2_ready = sem("cols2_ready")
        ga_ready = sem("ga_ready")
        gb_ready = sem("gb_ready")
        bounds_in = sem("bounds_in")
        bounds_out = sem("bounds_out")
        dve_step = sem("dve_step")
        pool_step = sem("pool_step")
        x_loaded = [sem(f"x_loaded{k}") for k in range(2)]
        mv_done = [sem(f"mv_done{k}") for k in range(2)]
        ve_done = [sem(f"ve_done{k}") for k in range(2)]
        rstd_done = [sem(f"rstd_done{k}") for k in range(2)]
        z_done = [sem(f"z_done{k}") for k in range(2)]
        t_done = [sem(f"t_done{k}") for k in range(2)]
        hT1_ready = sem("hT1_ready")
        x_copied = sem("x_copied")
        xg_ready = sem("xg_ready")
        attn_done = sem("attn_done")
        pair_free = sem("pair_free")
        x1_ready = sem("x1_ready")
        x1_stored = [sem(f"x1_stored{k}") for k in range(2)]
        hf_ready = sem("hf_ready")
        hi_ready = sem("hi_ready")
        lo_ready = sem("lo_ready")
        h_stored = [sem(f"h_stored{k}") for k in range(2)]
        unit_loaded = [sem(f"unit_loaded{k}") for k in range(NS)]
        unit_turned = sem("unit_turned")
        unit_cast = sem("unit_cast")
        dn_loaded = sem("dn_loaded")
        dn_turned = sem("dn_turned")
        dn_cast = sem("dn_cast")
        ht_loaded = sem("ht_loaded")
        gu_done = sem("gu_done")
        silu_done = sem("silu_done")
        h2_done = sem("h2_done")
        h2hi_done = sem("h2hi_done")
        down_done = sem("down_done")
        down_read = sem("down_read")
        tmp_ready = sem("tmp_ready")
        scaled = sem("scaled")
        res_ready = sem("res_ready")
        x1_loaded = [sem(f"x1_loaded{k}") for k in range(4)]
        res_stored = [sem(f"res_stored{k}") for k in range(4)]

        SLOT = [0, 1, 2] * 3 + [3, 4, 5]
        PIECE_COUNT = [16 * (m // NM + 1) for m in range(3 * NM)] + [16] * 3
        DVE_SUMMED = {0: 2, 2: 4, 3: 6, 4: 7, 5: 8, 6: 10, 8: 12, 10: 13, 11: 14}
        POOL_SUMMED = {1: 2, 7: 4, 9: 6}
        UNIT_INC = 16 * A
        ND = FC * (D // P) + 1
        primed = (h2_done, res_ready, dn_turned, dn_cast, down_read)
        PRIMED = 1
        NCONST = 12
        block = ctx.enter_context(nc.Block())

        class Tile:
            def __init__(self, j, o):
                self.j, self.o = j, o
                self.n, self.half, self.par = 2 * j + o, j + o // 2, o % 2

            def __add__(self, d):
                return Tile(self.j, self.o + d)

        LAST = NT - 1
        FIRST_LOOPED, PAIRS = 5, (NT - 8) // 2

        def static(t, lo, hi):
            return not isinstance(t.n, int) or lo <= t.n <= hi

        def each_tile(eng, step, first=0):
            for i in range(first, FIRST_LOOPED):
                step(Tile(0, i))
            with eng.Fori(0, PAIRS) as j:
                step(Tile(j, FIRST_LOOPED))
                step(Tile(j, FIRST_LOOPED + 1))
            for i in range(FIRST_LOOPED + 2 * PAIRS, NT + 1):
                step(Tile(0, i))

        def units(t):
            if static(t, 2, LAST):
                for s in range(NS):
                    r = NS * (t.o - 2) + s
                    yield s, 2 * NS * t.j + r, NS * t.j + r // 2, r % 2
            if not static(t, 0, LAST - 1) and static(t, 0, LAST):
                yield 0, NS * (NT - 2), FT, 0
        NU = 2 * FT + 1
        assert NS * (NT - 2) == 2 * FT

        def trailing(t):
            return {0: [], 1: [], 2: [], 3: [Tile(0, 0)], 4: [Tile(0, 1), Tile(0, 2)]}.get(t.n if isinstance(t.n, int) else None, [t + (-2)])

        def mask_quarter(eng, q):
            w = wst[q % 2].rearrange("p (b i) -> p b i", i=Q)
            bits = msum[q].rearrange("p (b o) -> p b o", o=1).to_broadcast([P, QB * KT, Q])
            eng.tensor_tensor(w, w, bits, ALU.mult).then_inc(w_masked[q % 2], 1)

        def halves_of(v, h, src):
            if v in (2, 5):
                return [(acc[v][:, h * H:(h + 1) * H], src)]
            by_tile = acc[v].rearrange("p (c a i) -> p a c i", c=KT, a=A)
            return [(by_tile[:, 2 * h + k], src[:, k * KA:(k + 1) * KA].rearrange("p (c i) -> p c i", c=KT))
                    for k in range(A // 2)]

        def wait_summed(eng, m):
            if m in DVE_SUMMED:
                eng.wait_ge(dve_summed, DVE_SUMMED[m])
            else:
                eng.wait_ge(pool_summed, POOL_SUMMED[m])

        @block.sync
        def _(sp):
            def load_x(t):
                sp.dma_start(xt[t.par], x_v[t.n]).then_inc(x_loaded[t.par], 16)

            def load_piece(m):
                if NM <= m < 3 * NM:
                    wait_summed(sp, m - NM)
                elif m == 3 * NM:
                    sp.wait_ge(mask_summed, NQ)
                dst = mp[SLOT[m]].rearrange("p (t n) -> p t n", t=KT)
                sp.dma_start(dst, mod_v[:, :, m * H:(m + 1) * H]).then_inc(piece_loaded[SLOT[m]], 16)

            def load_units(t):
                for s, u, c, g in units(t):
                    if static(t, 3, NT):
                        sp.wait_ge(unit_turned, u - NS + 1)
                    dst = stg[s].rearrange("p (b k) -> p b k", b=A)
                    for a in range(A):
                        rows = slice(Q * a, Q * (a + 1))
                        if isinstance(c, int) and c == FT:
                            for gg in range(2):
                                sp.dma_start(dst[rows, 2 * gg:2 * gg + 2], gu_l[gg][a]).then_inc(unit_loaded[s], 16)
                        else:
                            sp.dma_start(dst[rows], gu_v[g][c, a]).then_inc(unit_loaded[s], 16)

            def load_mask(q):
                if q >= 2:
                    sp.wait_ge(mask_summed, q - 1)
                for a in range(A):
                    sp.dma_start(mst[q % 2].rearrange("p (b k) -> p b k", b=QB)[Q * a:Q * (a + 1)], m_v[q, a])\
                      .then_inc(m_loaded[q % 2], 16)

            def load_weight(q):
                if q >= 2:
                    sp.wait_ge(w_turned[q % 2], 1)
                for a in range(A):
                    sp.dma_start(wst[q % 2].rearrange("p (b k) -> p b k", b=QB)[Q * a:Q * (a + 1)], w_v[q, a])\
                      .then_inc(w_loaded[q % 2], 16)

            sp.wait_ge(consts_set, 1)
            sp.dma_start(cvec, c_in.rearrange("o (p t) -> (o p) t", p=P)).then_inc(c_loaded, 16)
            load_x(Tile(0, 0))
            load_piece(0)
            load_piece(1)
            load_x(Tile(0, 1))
            load_piece(2)
            load_piece(3)
            for pair in range(NQ // 2):
                for q in (2 * pair, 2 * pair + 1):
                    load_mask(q)
                for q in (2 * pair, 2 * pair + 1):
                    load_weight(q)
            load_piece(4)
            load_piece(5)
            for i in range(2):
                sp.wait_ge(x_copied, i + 1)
                sp.wait_ge(z_done[0], i + 1)
                load_x(Tile(0, i + 2))
            for m in range(6, 10):
                load_piece(m)

            def step(t):
                if static(t, 1, LAST - 3):
                    sp.wait_ge(z_done[0], t.n + 2)
                    sp.wait_ge(xg_ready, t.n + 2)
                    load_x(t + 3)
                if static(t, 1, LAST - 1):
                    load_units(t + 1)

            each_tile(sp, step, 1)
            def load_h(b):
                sp.dma_start(hT_in, h_blk[b].rearrange("p t e -> p t e")).then_inc(ht_loaded, 16)

            sp.wait_ge(unit_turned, NU)
            sp.wait_ge(xg_ready, NT)
            for k in range(2):
                sp.wait_ge(h_stored[k], 16 * (BT // 2))
            load_h(0)
            sp.wait_ge(attn_done, NT)
            sp.wait_ge(z_done[0], NT)
            load_piece(10)
            load_piece(11)
            sp.wait_ge(t_done[0], NT)
            sp.dma_start(ds, down_s.rearrange("n o -> o n").to_broadcast([P, D])).then_inc(ds_loaded, 16)
            sp.wait_ge(unit_cast, NU)

            def load_dn(v, dq, fq):
                sp.wait_ge(dn_turned, v + PRIMED)
                for a in range(A):
                    dst = dstg[Q * a:Q * (a + 1), 0:DC].rearrange("p (b k) -> p b k", b=A)
                    sp.dma_start(dst, dn_v[dq, fq, a]).then_inc(dn_loaded, 16)

            with sp.Fori(0, D // P) as dq:
                for fq in range(FC):
                    load_dn(FC * dq + fq, dq, fq)
            sp.wait_ge(dn_turned, ND - 1 + PRIMED)
            for a in range(A):
                dst = dstg[Q * a:Q * (a + 1), :].rearrange("p (b k) -> p b k", k=Q)
                sp.dma_start(dst, dn_l[a % 2]).then_inc(dn_loaded, 16)
            sp.wait_ge(dn_cast, ND + PRIMED)

            G = 2 * BT
            def load_x1(b, g):
                if not isinstance(b, int) or b or g >= 4:
                    sp.wait_ge(res_stored[g % 4], 32 * b + 16 * (g // 4))
                sp.dma_start(io[g % 4], x1_d[BT * b + g // 2, :, (g % 2) * H:(g % 2 + 1) * H])\
                  .then_inc(x1_loaded[g % 4], 16)

            def store_block(b, last):
                for k in range(2):
                    sp.wait_ge(x1_stored[k], 16 * NT // 2)
                for g in range(4):
                    load_x1(b, g)
                if not last:
                    sp.wait_ge(gu_done, NF * b + NF)
                    for k in range(2):
                        sp.wait_ge(h_stored[k], 16 * NT // 2)
                    load_h(b + 1)
                for g in range(G):
                    sp.wait_ge(res_ready, G * b + g + 1 + PRIMED)
                    sp.dma_start(out_v[BT * b + g // 2, :, (g % 2) * H:(g % 2 + 1) * H], io[g % 4])\
                      .then_inc(res_stored[g % 4], 16)
                    if g < 4:
                        load_x1(b, g + 4)
            store_block(0, False)
            with sp.Fori(1, NB - 1) as b:
                store_block(b, False)
            store_block(NB - 1, True)
            for k in range(4):
                sp.wait_ge(res_stored[k], 16 * (2 * NT // 4))

        @block.gpsimd
        def _(pool):
            pool.memset(small[:, :], 0.0).then_inc(consts_set, 1)
            pool.memset(ident, 0.0).then_inc(consts_set, 1)
            pool.memset(blk1, 0.0).then_inc(consts_set, 1)
            pool.wait_ge(consts_set, 3)
            pool.affine_select(out=ident, in_=ident, compare_op=ALU.not_equal, fill=1.0, base=0,
                               pattern=[[-1, P]], channel_multiplier=1).then_inc(consts_set, 1)
            for a in range(A):
                r = slice(Q * a, Q * (a + 1))
                pool.wait_ge(consts_set, 4 + a)
                pool.memset(blk1[r, r], 1.0).then_inc(consts_set, 1)
            pool.wait_ge(consts_set, 8)
            for v, value in ((mhalf, -0.5), (eps, EPS), (one, 1.0), (two, 2.0)):
                pool.memset(v, value).then_inc(consts_set, 1)
            pool.wait_ge(consts_set, NCONST)
            for k, s in enumerate(primed):
                pool.memset(spare[:, k:k + 1], 0.0).then_inc(s, PRIMED)

            steps = [0]

            def link(*ins):
                for i in ins:
                    i.then_inc(pool_step, 1)
                steps[0] += len(ins)
                pool.wait_ge(pool_step, steps[0])

            def rstd_of(L, n):
                pool.wait_ge(mv_done[L], n + 1)
                pool.tensor_tensor(ve[L], mv[L][:, 1:2], eps, ALU.add).then_inc(ve_done[L], 1)
                pool.wait_ge(ve_done[L], n + 1)
                pool.tensor_tensor(rstd[L], ve[L], mhalf, ALU.pow).then_inc(rstd_done[L], 1)

            def add_bias(t):
                pool.wait_ge(x_loaded[t.par], 16 * t.half + 16)
                pool.tensor_tensor(xg[t.par], xt[t.par], gab, ALU.add).then_inc(xg_ready, 1)

            rstd_of(0, 0)
            pool.tensor_copy(xg[0], xt[0]).then_inc(x_copied, 1)
            rstd_of(0, 1)
            pool.tensor_copy(xg[1], xt[1]).then_inc(x_copied, 1)
            def sum_right(v):
                pool.wait_ge(piece_scaled, {0: 1, 3: 2, 4: 3}[v])
                if v in (3, 4):
                    pool.wait_ge(acc_used, v - 1)
                w = mp[SLOT[2 * v + 1]].rearrange("p (t n) -> p t n", t=KT)
                n = KT // 2
                while n > 1:
                    link(pool.tensor_tensor(w[:, 0:n], w[:, 0:n], w[:, n:2 * n], ALU.add))
                    n //= 2
                for (dst, a), (_, b) in zip(halves_of(v, 1, w[:, 0]), halves_of(v, 1, w[:, 1])):
                    pool.tensor_tensor(dst, a, b, ALU.add).then_inc(pool_summed, 1)

            sum_right(0)
            for q in range(0, NQ, 2):
                pool.wait_ge(mask_bits, q + 1)
                pool.wait_ge(w_loaded[0], A * 16 * (q // 2 + 1))
                mask_quarter(pool, q)

            def lo_part(r):
                pool.wait_ge(hi_ready, r.n + 1)
                pool.tensor_tensor(hs[r.par][:, 1, :], hf, hs[r.par][:, 0, :], ALU.subtract).then_inc(lo_ready, 1)
                pool.wait_ge(lo_ready, r.n + 1)
                pool.dma_start(h_d[r.n], hs[r.par].rearrange("p s e -> p (s e)")).then_inc(h_stored[r.par], 16)

            def step(t):
                tile = t.n if isinstance(t.n, int) else None
                if tile == 3:
                    pool.wait_ge(bounds_in, 4)
                    pool.partition_all_reduce(bma, bmx, P, bass.bass_isa.ReduceOp.max).then_inc(bounds_out, 1)
                if static(t, 0, LAST - 2):
                    rstd_of(0, t.n + 2)
                if tile in (1, 2):
                    sum_right(tile + 2)
                if tile == 0:
                    pool.wait_ge(ga_ready, 1)
                    pool.wait_ge(x_copied, 2)
                    for i in range(2):
                        pool.tensor_tensor(xg[i], xg[i], gab, ALU.add).then_inc(xg_ready, 1)
                for r in trailing(t):
                    lo_part(r)
                if static(t, 0, LAST):
                    rstd_of(1, t.n)
                    pool.wait_ge(x1_ready, t.n + 1)
                if static(t, 0, LAST - 2):
                    add_bias(t + 2)
                if static(t, 0, LAST):
                    pool.dma_start(x1_d[t.n], x1[t.par]).then_inc(x1_stored[t.par], 16)

            each_tile(pool, step)
            lo_part(Tile(0, LAST))

            def finish(q, k, loaded):
                pool.wait_ge(down_read, q + 1 + PRIMED)
                pool.tensor_tensor(tmp, tmp, gbs[:, (k % 2) * H:(k % 2 + 1) * H], ALU.mult).then_inc(scaled, 1)
                pool.wait_ge(scaled, q + 1)
                pool.wait_ge(x1_loaded[k], loaded)
                pool.tensor_tensor(io[k], tmp, io[k], ALU.add).then_inc(res_ready, 1)

            pool.wait_ge(gb_ready, 1)
            with pool.Fori(0, 2 * NB) as r:
                for k in range(4):
                    finish(4 * r + k, k, 16 * r + 16)

        @block.scalar
        def _(act):
            act.wait_ge(consts_set, NCONST)
            act.wait_ge(c_loaded, 16)
            act.activation(csil, cvec, ACT.Silu).then_inc(silu_c_done, 1)
            def scale_right(v):
                m = 2 * v + 1
                act.wait_ge(piece_loaded[SLOT[m]], PIECE_COUNT[m])
                w = mp[SLOT[m]].rearrange("p (t n) -> p t n", t=KT)
                for t in range(KT):
                    last = act.activation(w[:, t], w[:, t], ACT.Copy, scale=csil[:, t:t + 1])
                last.then_inc(piece_scaled, 1)

            act.wait_ge(silu_c_done, 1)
            scale_right(0)
            act.wait_ge(acc_used, 2)
            act.activation(colm[:, 0:KT], colp[:, 0:KT], ACT.Copy).then_inc(cols1_ready, 1)
            act.activation(colm[:, KT:2 * KT], colp[:, KT:2 * KT], ACT.Copy, bias=1.0).then_inc(cols1_ready, 1)
            act.wait_ge(cols1_ready, 2)

            def shift_scale(dst, src, L):
                for c in range(KT):
                    last = act.activation(dst[:, c, :], src[:, c, :], ACT.Identity,
                                          scale=colm[:, (2 * L + 1) * KT + c:(2 * L + 1) * KT + c + 1],
                                          bias=colm[:, 2 * L * KT + c:2 * L * KT + c + 1])
                return last

            z1T_c = z1T.rearrange("p h (c t) -> p (h c) t", t=P)
            z2T_c = z2T.rearrange("p h (c t) -> p (h c) t", t=P)
            hf_c = hf.rearrange("p (c t) -> p c t", c=KT)

            def turn_out(t):
                act.wait_ge(t_done[0], t.n + 1)
                if static(t, 2, NT):
                    act.wait_ge(attn_done, t.n - 1)
                shift_scale(hT1[t.par], z1T_c, 0).then_inc(hT1_ready, 1)

            turn_out(Tile(0, 0))
            act.dma_start(gab, bias.rearrange("(o n) -> o n", o=1).to_broadcast([P, D])).then_inc(bias_loaded, 16)
            for s_in, s_col, r in ((gate_s, sgs, 0), (up_s, sus, P // 2)):
                for a in range(A):
                    src = s_in[FA * a:FA * (a + 1), :].rearrange("(c i) o -> i (c o)", i=Q)
                    act.dma_start(s_col[Q * a:Q * (a + 1), 0:FT], src).then_inc(scales_loaded, 16)
                act.dma_start(s_col[r:r + FL, FT:NF], s_in[FT * P:F, :]).then_inc(scales_loaded, 16)

            def cast_units(t):
                for s, u, c, g in units(t):
                    act.wait_ge(unit_turned, u + 1)
                    act.activation(wgu_u[:, 2 * c + g, :], trn[s], ACT.Copy).then_inc(unit_cast, 1)

            def second_input(r):
                act.wait_ge(t_done[1], r.n + 1)
                if static(r, 1, NT):
                    act.wait_ge(lo_ready, r.n)
                shift_scale(hf_c, z2T_c, 1).then_inc(hf_ready, 1)
                act.wait_ge(hf_ready, r.n + 1)
                if static(r, 2, NT):
                    act.wait_ge(h_stored[r.par], 16 * r.half)
                act.activation(hs[r.par][:, 0, :], hf, ACT.Copy).then_inc(hi_ready, 1)

            def step(t):
                tile = t.n if isinstance(t.n, int) else None
                if static(t, 0, LAST - 1):
                    turn_out(t + 1)
                if tile in (1, 2):
                    scale_right(tile + 2)
                if tile == 2:
                    for k in range(2):
                        act.wait_ge(w_turned[k], NQ // 2)
                if tile == 3:
                    act.wait_ge(cols2_ready, 2)
                    second_input(Tile(0, 0))
                elif tile == 4:
                    second_input(Tile(0, 1))
                    cast_units(Tile(0, 3))
                    second_input(Tile(0, 2))
                    wait_summed(act, 9)
                    cast_units(t)
                else:
                    cast_units(t)
                    for r in trailing(t):
                        second_input(r)

            each_tile(act, step)

            def tile_out(n, c, k):
                act.wait_ge(gu_done, n + 1)
                act.wait_ge(h2_done, n + PRIMED)
                act.activation(silu, pA[:, 2 * k, :], ACT.Silu, scale=sgs[:, bass.ds(c, 1)]).then_inc(silu_done, 1)
                act.wait_ge(h2_done, n + 1 + PRIMED)
                act.activation(h2[:, 0, c, :], pA[:, 2 * k + 1, :], ACT.Copy, scale=1.0 / LO).then_inc(h2hi_done, 1)

            def last_tile_out(n):
                k, lo_h, up_h = 2 * ((NF - 1) % 2), slice(0, FL), slice(FL, P)
                act.wait_ge(gu_done, n + 1)
                act.wait_ge(h2_done, n + PRIMED)
                act.activation(silu[up_h], pA[lo_h, k, :], ACT.Silu, scale=sgs[lo_h, FT:NF]).then_inc(silu_done, 1)
                act.wait_ge(h2_done, n + 1 + PRIMED)
                act.activation(h2[lo_h, 0, FT, :], pA[up_h, k, :], ACT.Copy, scale=1.0 / LO)
                act.activation(h2[up_h, 0, FT, :], pA[up_h, k, :], ACT.Copy, scale=1.0 / LO).then_inc(h2hi_done, 1)

            def dn_out(v, dq, fq):
                act.wait_ge(dn_turned, v + 1 + PRIMED)
                dst = wd[:, CF * fq:CF * (fq + 1), bass.ds(P * dq, P)]
                act.activation(dst, dtrn[:, 0:DC].rearrange("p (c d) -> p c d", c=CF), ACT.Copy).then_inc(dn_cast, 1)

            def last_dn_out():
                act.wait_ge(dn_turned, ND + PRIMED)
                act.activation(wd[0:FL, FT, :], dtrn[0:FL, :], ACT.Copy)
                act.activation(wd[FL:P, FT, :], dtrn[FL:P, :], ACT.Copy, scale=1.0 / LO).then_inc(dn_cast, 1)

            def out_half(q, k):
                act.wait_ge(down_done, q + 1)
                act.wait_ge(res_ready, q + PRIMED)
                act.activation(tmp, pB[:, 2 * k, :], ACT.Copy).then_inc(tmp_ready, 1)

            def down_out(b):
                with act.Fori(0, BT) as ts:
                    for k in range(2):
                        out_half(2 * BT * b + 2 * ts + k, k)

            tile_out(0, 0, 0)
            second_input(Tile(0, LAST))
            tile_out(1, 1, 1)
            for k in range(2):
                act.wait_ge(x1_stored[k], 16 * NT // 2)
                act.wait_ge(h_stored[k], 16 * NT // 2)
            act.wait_ge(gb_ready, 1)
            with act.Fori(0, D // P) as j:
                for k in range(2):
                    tile_out(2 * j + 2 + k, 2 * j + 2 + k, k)
                for fq in range(FC):
                    dn_out(FC * j + fq, j, fq)
            for c in range(2 * (D // P) + 2, FT - 1):
                tile_out(c, c, c % 2)
            tile_out(FT - 1, FT - 1, 0)
            last_dn_out()
            last_tile_out(FT)
            down_out(0)
            with act.Fori(1, NB) as b:
                with act.Fori(0, FT // 2) as j:
                    for k in range(2):
                        tile_out(NF * b + 2 * j + k, 2 * j + k, k)
                tile_out(NF * b + FT - 1, FT - 1, 0)
                last_tile_out(NF * b + FT)
                down_out(b)

        @block.tensor
        def _(pe):
            def transpose(L, t):
                z, dst, taken = ((z1, z1T, hT1_ready), (z2, z2T, hf_ready))[L]
                zc = z.rearrange("p (c k) -> p c k", c=KT)
                pe.wait_ge(z_done[L], t.n + 1)
                if static(t, 1, NT):
                    pe.wait_ge(taken, t.n)
                for c in range(KT):
                    last = pe.transpose(dst[:, c // 4, (c % 4) * P:(c % 4 + 1) * P], zc[:, c], ident)
                last.then_inc(t_done[L], 1)

            def attend(t, h, ks=range(KT)):
                if h == 0:
                    pe.wait_ge(hT1_ready, t.n + 1)
                    if static(t, 2, NT):
                        pe.wait_ge(pair_free, t.n - 1)
                for c in ks:
                    last = pe.matmul(pA[:, 2 * t.par + h, :], hT1[t.par][:, c, :], wT[:, c, h * H:(h + 1) * H],
                                     start=(c == 0), stop=(c == KT - 1))
                if h == 1:
                    last.then_inc(attn_done, 1)

            def columns(v, dst):
                for h in range(2):
                    wait_summed(pe, 2 * v + h)
                for c in range(KT):
                    last = pe.matmul(dst[:, c:c + 1], acc[v][:, P * c:P * (c + 1)], one, start=True, stop=True)
                last.then_inc(acc_used, 1)

            def gate_row(v, dst):
                for h in range(2):
                    wait_summed(pe, 2 * v + h)
                for h in range(2):
                    last = pe.matmul(dst[:, h * H:(h + 1) * H], two.to_broadcast([P, P]), acc[v][:, h * H:(h + 1) * H],
                                     start=True, stop=True)
                last.then_inc(acc_used, 1)

            def mask_total_of(q):
                pe.wait_ge(mask_summed, q + 1)
                pe.matmul(sump[q], blk1, msum[q], start=True, stop=True).then_inc(mask_total, 1)

            pe.wait_ge(consts_set, NCONST)
            transpose(0, Tile(0, 0))
            columns(0, colp[:, 0:KT])
            mask_total_of(0)
            mask_total_of(1)
            columns(1, colp[:, KT:2 * KT])
            for k in range(2):
                pe.wait_ge(w_turned[k], 1)
            attend(Tile(0, 0), 0, range(KT // 2))
            mask_total_of(2)
            mask_total_of(3)
            attend(Tile(0, 0), 0, range(KT // 2, KT))
            transpose(0, Tile(0, 1))
            attend(Tile(0, 1), 0)
            for k in range(2):
                pe.wait_ge(w_turned[k], 2)
            attend(Tile(0, 0), 1)
            gate_row(2, rowp[0])
            transpose(0, Tile(0, 2))
            attend(Tile(0, 1), 1)

            def step(t):
                tile = t.n if isinstance(t.n, int) else None
                if static(t, 0, LAST):
                    attend(t, 0)
                if static(t, 0, LAST - 1):
                    transpose(0, t + 1)
                if tile == 4:
                    transpose(1, Tile(0, 1))
                elif tile != 3:
                    transpose(1, t + (-2))
                if tile == 4:
                    pe.wait_ge(cols2_copied, 1)
                if static(t, 0, LAST):
                    attend(t, 1)
                if tile == 3:
                    pe.wait_ge(pair_free, 3)
                    for v in (3, 4):
                        columns(v, colp2[:, KT * (v - 3):KT * (v - 2)])
                if tile == 4:
                    transpose(1, Tile(0, 2))

            each_tile(pe, step, 2)

            def gate_up(b, n, c, k):
                pe.wait_ge(ht_loaded, 16 * b + 16)
                pe.wait_ge(pair_free, NT + n - 1)
                for g in range(2):
                    for kc in range(KT):
                        for s in range(2):
                            last = pe.matmul(pA[:, 2 * k + g, :], wgu_u[:, 2 * c + g, P * kc:P * (kc + 1)], hT[:, s, kc],
                                             start=(kc == 0 and s == 0), stop=(kc == KT - 1 and s == 1))
                last.then_inc(gu_done, 1)

            def last_gate_up(n):
                pe.wait_ge(pair_free, NT + n - 1)
                for kc in range(KT):
                    for s in range(2):
                        last = pe.matmul(pA[:, 2 * ((NF - 1) % 2), :], wgu_u[:, 2 * FT, P * kc:P * (kc + 1)], hT[:, s, kc],
                                         start=(kc == 0 and s == 0), stop=(kc == KT - 1 and s == 1))
                last.then_inc(gu_done, 1)

            def down(b, ts, k):
                q = 2 * BT * b + 2 * ts + k
                pe.wait_ge(pair_free, NT + NF * b + FT)
                for c in range(FT):
                    for s in range(2):
                        pe.matmul(pB[:, 2 * k + s, :], h2[:, s, c, bass.ds(P * ts, P)], wd[:, c, k * H:(k + 1) * H],
                                  start=(c == 0), stop=(c == FT - 1 and s == 1))
                pe.wait_ge(pair_free, NT + NF * b + NF)
                pe.matmul(pB[:, 2 * k, :], h2[:, 0, FT, bass.ds(P * ts, P)], wd[:, FT, k * H:(k + 1) * H],
                          start=False, stop=True).then_inc(down_done, 1)
                pe.wait_ge(down_read, q + PRIMED)

            def ffn_block(b, first):
                pe.wait_ge(unit_cast, NU)
                if first:
                    gate_up(b, 0, 0, 0)
                    transpose(1, Tile(0, LAST))
                    gate_up(b, 1, 1, 1)
                    gate_row(5, rowp[1])
                with pe.Fori(1 if first else 0, FT // 2) as j:
                    for k in range(2):
                        gate_up(b, NF * b + 2 * j + k, 2 * j + k, k)
                gate_up(b, NF * b + FT - 1, FT - 1, 0)
                last_gate_up(NF * b + FT)
                pe.wait_ge(hf_ready, NT)
                pe.wait_ge(gb_ready, 1)
                pe.wait_ge(dn_cast, ND + PRIMED)
                with pe.Fori(0, BT) as ts:
                    for k in range(2):
                        down(b, ts, k)

            ffn_block(0, True)
            with pe.Fori(1, NB) as b:
                ffn_block(b, False)

        @block.vector
        def _(dve):
            steps = [0]

            def link(*ins):
                for i in ins:
                    i.then_inc(dve_step, 1)
                steps[0] += len(ins)
                dve.wait_ge(dve_step, steps[0])

            def stats(L, n, src):
                for h in range(2):
                    dve.bn_stats(bnst[L][:, 6 * h:6 * h + 6], src[:, h * H:(h + 1) * H])
                dve.drain()
                dve.bn_aggr(mv[L], bnst[L]).then_inc(mv_done[L], 1)

            def normalise(L, t):
                z, src = ((z1, xt[t.par]), (z2, x1[t.par]))[L]
                dve.wait_ge(rstd_done[L], t.n + 1)
                if static(t, 1, NT):
                    dve.wait_ge(t_done[L], t.n)
                dve.tensor_scalar(z.rearrange("p (c a i) -> p a c i", c=KT, a=A),
                                  src.rearrange("p (a c i) -> p a c i", c=KT, a=A),
                                  mv[L][:, 0:1], rstd[L], ALU.subtract, ALU.mult).then_inc(z_done[L], 1)

            def norm1(t):
                dve.wait_ge(x_loaded[t.par], 16 * t.half + 16)
                stats(0, t.n, xt[t.par])
                normalise(0, t)

            def residual(t):
                dve.wait_ge(attn_done, t.n + 1)
                if static(t, 2, NT):
                    dve.wait_ge(x1_stored[t.par], 16 * t.half)
                ps = pA[:, 2 * t.par:2 * t.par + 2, :].rearrange("p h n -> p (h n)")
                dve.tensor_tensor(x1[t.par], ps, ga, ALU.mult).then_inc(pair_free, 1)
                dve.wait_ge(pair_free, t.n + 1)
                dve.wait_ge(xg_ready, t.n + 1)
                dve.tensor_tensor(x1[t.par], x1[t.par], xg[t.par], ALU.add).then_inc(x1_ready, 1)
                dve.wait_ge(x1_ready, t.n + 1)
                stats(1, t.n, x1[t.par])

            def turn_units(t):
                for s, u, c, g in units(t):
                    dve.wait_ge(unit_loaded[s], UNIT_INC * (t.n - 1) if not (isinstance(c, int) and c == FT)
                                else UNIT_INC * (NT - 2) + 2 * UNIT_INC)
                    if static(t, 3, NT):
                        dve.wait_ge(unit_cast, u - NS + 1)
                    dve.transpose(trn[s].rearrange("p (c b i) -> p c b i", c=KT, b=A),
                                  stg[s].rearrange("p (b c i) -> p c b i", b=A, c=KT)).then_inc(unit_turned, 1)

            def clamp_gate(dst, tmp_row, src):
                link(dve.tensor_scalar(tmp_row, src, 0.0, -0.5, ALU.is_ge, ALU.add))
                link(dve.tensor_scalar(dst.bitcast(I32), src.bitcast(I32), 0x7FFFFFFF, None, ALU.bitwise_and))
                link(dve.scalar_tensor_tensor(out=dst, in0=dst, scalar=2 * GATE_FLOOR, in1=tmp_row,
                                              op0=ALU.max, op1=ALU.mult))

            def sum_half(v, h):
                m = 2 * v + h
                dve.wait_ge(piece_loaded[SLOT[m]], PIECE_COUNT[m])
                if v in (2, 3, 4):
                    dve.wait_ge(acc_used, v - 1)
                w = mp[SLOT[m]].rearrange("p (t n) -> p t n", t=KT)
                link(*[dve.tensor_scalar(dst, src, csil[:, 0:1], None, ALU.mult) for dst, src in halves_of(v, h, w[:, 0])])
                for t in range(1, KT):
                    sums = [dve.scalar_tensor_tensor(out=dst, in0=src, scalar=csil[:, t:t + 1], in1=dst,
                                                     op0=ALU.mult, op1=ALU.add) for dst, src in halves_of(v, h, w[:, t])]
                    if t < KT - 1:
                        link(*sums)
                for i in sums:
                    i.then_inc(dve_summed, 1)

            def mask_sums(q):
                dve.wait_ge(m_loaded[q % 2], A * 16 * (q // 2 + 1))
                dve.tensor_reduce(msum[q], mst[q % 2].rearrange("p (b i) -> p b i", i=Q), AXX, ALU.add)\
                   .then_inc(mask_summed, 1)

            dve.wait_ge(consts_set, NCONST)
            norm1(Tile(0, 0))
            dve.wait_ge(silu_c_done, 1)
            sum_half(0, 0)
            norm1(Tile(0, 1))
            for h in range(2):
                sum_half(1, h)
            def mask_of(q):
                dve.wait_ge(mask_total, q + 1)
                dve.tensor_scalar(msum[q], sump[q], 0.0, None, ALU.is_gt).then_inc(mask_bits, 1)

            def turn_quarter(q):
                dve.wait_ge(w_masked[q % 2], q // 2 + 1)
                dve.transpose(wT[:, :, QB * Q * q:QB * Q * (q + 1)].rearrange("p c (b i) -> p c b i", i=Q),
                              wst[q % 2].rearrange("p (b c i) -> p c b i", b=QB, c=KT)).then_inc(w_turned[q % 2], 1)

            for pair in range(NQ // 2):
                even, odd = 2 * pair, 2 * pair + 1
                mask_sums(even)
                mask_sums(odd)
                mask_of(even)
                mask_of(odd)
                dve.wait_ge(mask_bits, odd + 1)
                dve.wait_ge(w_loaded[1], A * 16 * (pair + 1))
                mask_quarter(dve, odd)
                turn_quarter(odd)
                turn_quarter(even)
            for h in range(2):
                sum_half(2, h)

            def gate_a():
                dve.wait_ge(acc_used, 3)
                clamp_gate(ga, x1[1], rowp[0])
                dve.wait_ge(bias_loaded, 16)
                dve.tensor_tensor(gab, gab, ga, ALU.mult).then_inc(ga_ready, 1)
                dve.wait_ge(ga_ready, 1)

            def scales():
                dve.wait_ge(acc_used, 5)
                dve.wait_ge(scales_loaded, 16 * 2 * (A + 1))
                s_b, one_cb = colm[:, 2 * KT:3 * KT], colm[:, 3 * KT:4 * KT]
                link(dve.tensor_copy(s_b, colp2[:, 0:KT]))
                dve.tensor_scalar(one_cb, colp2[:, KT:2 * KT], 1.0, None, ALU.add).then_inc(cols2_copied, 1)
                dve.wait_ge(cols2_copied, 1)
                for k, v in enumerate((one_cb, s_b, sgs, sus)):
                    m = mag[:, 0:v.shape[1]]
                    link(dve.scalar_tensor_tensor(out=m, in0=v, scalar=-1.0, in1=v, op0=ALU.mult, op1=ALU.max))
                    dve.tensor_reduce(bmx[:, k:k + 1], m, AXX, ALU.max).then_inc(bounds_in, 1)
                    dve.wait_ge(bounds_in, k + 1)
                dve.wait_ge(bounds_out, 1)
                b1, g1, p1, s1, i1, b2, u2, p2, s2, i2 = (sc[:, k:k + 1] for k in range(10))

                def power(bound, p, s, inv):
                    link(dve.tensor_scalar(bound, bound, 2.0 ** -60, 2.0 ** 60, ALU.max, ALU.min))
                    link(dve.tensor_scalar(p.bitcast(I32), bound.bitcast(I32), 0x7F800000, None, ALU.bitwise_and))
                    link(dve.tensor_scalar(s.bitcast(I32), p.bitcast(I32), -1.0, float((2 * 127 + 14) << 23),
                                           ALU.mult, ALU.add))
                    link(dve.tensor_scalar(inv, p, 2.0 ** -14, None, ALU.mult))

                link(dve.tensor_scalar(b1, bma[:, 0:1], bma[:, 1:2], float(D) ** 0.5, ALU.add, ALU.mult))
                link(dve.tensor_scalar(g1, b1, float(D) ** 0.5 * W_MAX, None, ALU.mult))
                power(b1, p1, s1, i1)
                link(dve.tensor_scalar(u2, g1, bma[:, 3:4], None, ALU.mult))
                link(dve.tensor_scalar(b2, g1, bma[:, 2:3], u2, ALU.mult, ALU.mult))
                power(b2, p2, s2, i2)
                link(dve.tensor_scalar(s2, s2, LO, None, ALU.mult))
                link(dve.tensor_scalar(sgs, sgs, i1, None, ALU.mult))
                link(dve.tensor_scalar(sus, sus, i1, s2, ALU.mult, ALU.mult))
                dve.tensor_scalar(one_cb, one_cb, s1, None, ALU.mult).then_inc(cols2_ready, 1)
                dve.tensor_scalar(s_b, s_b, s1, None, ALU.mult).then_inc(cols2_ready, 1)

            def gate_b():
                dve.wait_ge(acc_used, 6)
                clamp_gate(gbs[:, :], sgn, rowp[1])
                dve.wait_ge(ds_loaded, 16)
                dve.scalar_tensor_tensor(out=gbs[:, :], in0=gbs[:, :], scalar=sc[:, 9:10], in1=ds,
                                         op0=ALU.mult, op1=ALU.mult).then_inc(gb_ready, 1)

            def step(t):
                tile = t.n if isinstance(t.n, int) else None
                late_units = tile in (2, 3, 4)
                if tile == 3:
                    scales()
                if not late_units:
                    turn_units(t)
                if static(t, 0, LAST - 2):
                    norm1(t + 2)
                if tile == 0:
                    gate_a()
                if tile == 2:
                    sum_half(4, 0)
                if static(t, 1, NT):
                    normalise(1, t + (-1))
                if static(t, 0, LAST):
                    residual(t)
                if late_units:
                    turn_units(t)
                if tile == 1:
                    sum_half(3, 0)

            each_tile(dve, step)
            def tile_out(n, c, k):
                dve.wait_ge(silu_done, n + 1)
                up = pA[:, 2 * k + 1, :]
                dve.scalar_tensor_tensor(out=up, in0=up, scalar=sus[:, bass.ds(c, 1)], in1=silu, op0=ALU.mult, op1=ALU.mult)\
                   .then_inc(h2_done, 1)
                dve.wait_ge(h2_done, n + 1 + PRIMED)
                dve.wait_ge(h2hi_done, n + 1)
                dve.scalar_tensor_tensor(out=h2[:, 1, c, :], in0=h2[:, 0, c, :], scalar=-LO, in1=up,
                                         op0=ALU.mult, op1=ALU.add).then_inc(pair_free, 1)

            def last_tile_out(n):
                up_h = slice(FL, P)
                dve.wait_ge(silu_done, n + 1)
                up = pA[up_h, 2 * ((NF - 1) % 2), :]
                dve.scalar_tensor_tensor(out=up, in0=up, scalar=sus[up_h, FT:NF], in1=silu[up_h], op0=ALU.mult,
                                         op1=ALU.mult).then_inc(h2_done, 1)
                dve.wait_ge(h2_done, n + 1 + PRIMED)
                dve.wait_ge(h2hi_done, n + 1)
                dve.scalar_tensor_tensor(out=h2[up_h, 0, FT, :], in0=h2[up_h, 0, FT, :], scalar=-LO, in1=up,
                                         op0=ALU.mult, op1=ALU.add).then_inc(pair_free, 1)

            def turn_dn(v):
                dve.wait_ge(dn_loaded, A * 16 * (v + 1))
                dve.wait_ge(dn_cast, v + PRIMED)
                dve.transpose(dtrn[:, 0:DC].rearrange("p (c b i) -> p c b i", c=CF, b=A),
                              dstg[:, 0:DC].rearrange("p (b c i) -> p c b i", b=A, c=CF)).then_inc(dn_turned, 1)

            def down_out(b):
                with dve.Fori(0, BT) as ts:
                    for k in range(2):
                        dve.wait_ge(tmp_ready, 2 * BT * b + 2 * ts + k + 1)
                        dve.scalar_tensor_tensor(out=tmp, in0=pB[:, 2 * k + 1, :], scalar=1.0 / LO, in1=tmp,
                                                 op0=ALU.mult, op1=ALU.add).then_inc(down_read, 1)

            sum_half(5, 0)
            tile_out(0, 0, 0)
            sum_half(5, 1)
            tile_out(1, 1, 1)
            gate_b()
            with dve.Fori(0, D // P) as j:
                for k in range(2):
                    tile_out(2 * j + 2 + k, 2 * j + 2 + k, k)
                for fq in range(FC):
                    turn_dn(FC * j + fq)
            for c in range(2 * (D // P) + 2, FT - 1):
                tile_out(c, c, c % 2)
            tile_out(FT - 1, FT - 1, 0)
            dve.wait_ge(dn_loaded, A * 16 * ND)
            dve.wait_ge(dn_cast, ND - 1 + PRIMED)
            dve.transpose(dtrn, dstg).then_inc(dn_turned, 1)
            last_tile_out(FT)
            down_out(0)
            with dve.Fori(1, NB) as b:
                with dve.Fori(0, FT // 2) as j:
                    for k in range(2):
                        tile_out(NF * b + 2 * j + k, 2 * j + k, k)
                tile_out(NF * b + FT - 1, FT - 1, 0)
                last_tile_out(NF * b + FT)
                down_out(b)


_INS = ['L0_attn_data', 'L0_attn_mask', 'L0_attn_weight', 'L0_attn_bias', 'L0_ffn_gate_w', 'L0_ffn_gate_s',
        'L0_ffn_up_w', 'L0_ffn_up_s', 'L0_ffn_down_w', 'L0_ffn_down_s', 'L0_c', 'L0_wmod']


def kernel(**inputs):
    import numpy as np
    import concourse.bacc as bacc
    from concourse.bass_utils import run_bass_kernel_spmd

    nc = bacc.Bacc("TRN2", target_bir_lowering=False, num_devices=1)
    arrays, args = {}, []
    for name in _INS:
        a = np.ascontiguousarray(inputs[name])
        arrays[f"in_{name}"] = a
        args.append(nc.dram_tensor(f"in_{name}", a.shape, mybir.dt.from_np(a.dtype), kind="ExternalInput").ap())
    shape = np.asarray(inputs['L0_attn_data']).shape
    out = nc.dram_tensor("out_0", shape, F32, kind="ExternalOutput").ap()
    adaln_kernel(nc, *args, out)
    r = run_bass_kernel_spmd(nc, [arrays], core_ids=[0])
    return r.results[0]["out_0"]
```

```python
from contextlib import ExitStack

import concourse.bass as bass
from concourse import mybir

F32 = mybir.dt.float32
F16 = mybir.dt.float16
I32 = mybir.dt.int32
ALU = mybir.AluOpType
ACT = mybir.ActivationFunctionType
AXX = mybir.AxisListType.X

P = 128
EPS = 1e-5
GATE_FLOOR = 0.25


def adaln_kernel(nc, data, mask, weight, bias, gate_w, gate_s, up_w, up_s, down_w, down_s, c_in, wmod, out):
    T, D = data.shape[1], data.shape[2]
    F = gate_w.shape[0]
    Q = 32
    A = P // Q
    KT = D // P
    KA = D // A
    NT = T // P
    H = 512
    FT = F // P
    FL = F - FT * P
    FA = FT * Q
    NF = FT + 1
    assert FL == P // 2 and NF % 2 == 0 and D == 2 * H and KA == KT * Q
    BT = H // P
    NB = T // H
    NQ = 4
    QB = D // Q // NQ
    FC = 3
    CF = FT // FC
    UNITS_AFTER = (1, 2, 1, 2)
    FIRST_DN = 3
    SMALL = 208
    LO = 2048.0
    W_MAX = 128.0

    x_v = data.rearrange("o (n p) d -> (o n) p d", p=P)
    out_v = out.rearrange("o (n p) d -> (o n) p d", p=P)
    x1_d = nc.dram_tensor("x1_scratch", (NT, P, D), F32).ap()
    h_d = nc.dram_tensor("h_scratch", (NT, P, 2 * D), F16).ap()
    h_blk = h_d.rearrange("(b t) p e -> b p t e", t=BT)
    w_v = weight.rearrange("(q b j) (a k) -> q a j b k", q=NQ, j=Q, a=A)
    m_v = mask.rearrange("(q b j) (a k) -> q a j b k", q=NQ, j=Q, a=A)
    gu_v = [w[0:FT * P, :].rearrange("(b q j) (a k) -> q a j b k", b=A, j=Q, a=A) for w in (gate_w, up_w)]
    gu_l = [w[FT * P:F, :].rearrange("(b j) (a k) -> a j b k", j=Q, a=A) for w in (gate_w, up_w)]
    dn_v = down_w[:, 0:FT * P].rearrange("(d b j) (a g k) -> d g a j b k", b=A, j=Q, a=A, g=FC)
    dn_l = down_w[:, FT * P:F].rearrange("(b j) (a k) -> a j b k", j=Q, k=Q)
    mod_v = wmod.rearrange("(p t) n -> p t n", p=P)

    with ExitStack() as ctx:
        ctx.enter_context(nc.allow_non_contiguous_dma(reason="the scales of the weights, once, 22 KB"))

        def sem(name):
            return ctx.enter_context(nc.semaphore(name))

        wgu = ctx.enter_context(nc.sbuf_tensor("wgu", [P, FT * 2 * D + D], F16))
        wgu_u = wgu[:, :].rearrange("p (u e) -> p u e", e=D)
        gbs = ctx.enter_context(nc.sbuf_tensor("gbs", [P, D], F32))
        small = ctx.enter_context(nc.sbuf_tensor("small", [P, SMALL], F32))
        ident = ctx.enter_context(nc.sbuf_tensor("ident", [P, P], F32))[:, :]
        WORK = nc.sbuf_bytes_remaining // 64 * 64
        work = ctx.enter_context(nc.sbuf_tensor("work", [P, WORK // 4], F32))
        top = [0, 0]

        def carve(phase, nbytes, dt=F32):
            o = top[phase]
            top[phase] = o + nbytes
            assert top[phase] <= WORK, (phase, top[phase], WORK)
            v = work[:, o // 4:(o + nbytes) // 4]
            return v if dt == F32 else v.bitcast(dt)

        wT = carve(0, 4 * KT * D).rearrange("p (c n) -> p c n", c=KT)
        hT1 = [carve(0, 4 * D).rearrange("p (c t) -> p c t", c=KT) for _ in range(2)]
        xt = [carve(0, 4 * D) for _ in range(2)]
        xg = [carve(0, 4 * D) for _ in range(2)]
        x1 = [carve(0, 4 * D) for _ in range(2)]
        z1 = carve(0, 4 * D)
        z2 = carve(0, 4 * D)
        hf = carve(0, 4 * D)
        hs = [carve(0, 4 * D, F16).rearrange("p (s e) -> p s e", s=2) for _ in range(2)]
        ga = carve(0, 4 * D)
        gab = carve(0, 4 * D)
        NS = 3
        stg = [carve(0, 4 * D, I32) for _ in range(NS)]
        trn = [carve(0, 4 * D, I32) for _ in range(NS)]
        h2 = carve(1, 2 * 2 * H * NF, F16).rearrange("p (s c t) -> p s c t", s=2, c=NF)
        wd = carve(1, 2 * NF * D, F16).rearrange("p (c d) -> p c d", c=NF)
        hT_in = carve(1, 2 * 2 * D * BT, F16).rearrange("p (t e) -> p t e", t=BT)
        hT = hT_in.rearrange("p t (s c k) -> p s c t k", s=2, c=KT)
        shared = top[1]
        io = [carve(1, 4 * H) for _ in range(4)]
        tmp = carve(1, 4 * H)
        DC = A * CF * Q
        top[1] = shared
        dlast, dlast_trn = [carve(1, 4 * D, I32) for _ in range(2)]
        top[1] = shared
        dstg = [carve(1, 4 * DC, I32) for _ in range(2)]
        dtrn = carve(1, 4 * DC, I32)
        silu = carve(1, 4 * H)
        pre = wgu[:, :].bitcast(F32)
        QE = QB * KA
        PIECE = KT * H
        NM = 3
        wst = [pre[:, QE * k:QE * (k + 1)] for k in range(2)]
        mst = [pre[:, QE * (2 + k):QE * (3 + k)].bitcast(I32) for k in range(2)]
        o = 4 * QE
        mp = [pre[:, o + PIECE * k:o + PIECE * (k + 1)] for k in range(NM)]
        mp.append(pre[:, o - PIECE:o])
        mp += [work[:, (NF * s + 4) * H // 2:(NF * s + 4) * H // 2 + PIECE] for s in range(2)]
        o += NM * PIECE
        acc_a = pre[:, o:o + D]
        blk1 = pre[:, o + D:o + D + P]
        o += D + P
        msum = [pre[:, o + QB * KT * q:o + QB * KT * (q + 1)] for q in range(NQ)]
        acc = [acc_a, hf, acc_a, hf, acc_a, gbs[:, :]]
        down_s_row = z1
        gb_sign = xt[1]

        used = [0]

        def cols(n):
            used[0] += n
            assert used[0] <= SMALL
            return small[:, used[0] - n:used[0]]

        cvec = cols(KT)
        csil = cols(KT)
        colm = cols(4 * KT)
        sgs = cols(NF)
        sus = cols(NF)
        mag = cols(NF)
        bnst = [cols(12) for _ in range(2)]
        mv = [cols(2) for _ in range(2)]
        ve = [cols(1) for _ in range(2)]
        rstd = [cols(1) for _ in range(2)]
        mhalf = cols(1)
        eps = cols(1)
        one = cols(1)
        two = cols(1)
        bmx = cols(4)
        bma = cols(4)
        b1, g1, p1, s1, i1, b2, u2, p2, s2, i2 = (cols(1) for _ in range(10))
        spare = cols(5)

        pA = ctx.enter_context(nc.psum_tensor("pA", [P, 4, H], F32))
        pB = ctx.enter_context(nc.psum_tensor("pB", [P, 4, H], F32))
        z1T, z2T = pB[:, 0:2, :], pB[:, 2:4, :]
        colp = pB[:, 2, 0:2 * KT]
        colp2 = pA[:, 1, 0:2 * KT]
        sump = [bank[:, 0:QB * KT] for bank in (pA[:, 2], pA[:, 3], pA[:, 1], pB[:, 3])]
        rowp = [pB[:, 2:4, :].rearrange("p h n -> p (h n)"),
                pB[:, 0:2, :].rearrange("p h n -> p (h n)")]

        consts_set = sem("consts_set")
        c_loaded = sem("c_loaded")
        silu_c_done = sem("silu_c_done")
        scales_loaded = sem("scales_loaded")
        bias_loaded = sem("bias_loaded")
        down_s_loaded = sem("down_s_loaded")
        piece_loaded = [sem(f"piece_loaded{k}") for k in range(NM + 3)]
        dve_summed = sem("dve_summed")
        pool_summed = sem("pool_summed")
        piece_scaled = sem("piece_scaled")
        acc_used = sem("acc_used")
        cols2_copied = sem("cols2_copied")
        m_loaded = [sem(f"m_loaded{k}") for k in range(2)]
        w_loaded = [sem(f"w_loaded{k}") for k in range(2)]
        mask_summed = sem("mask_summed")
        mask_total = sem("mask_total")
        mask_bits = sem("mask_bits")
        w_masked = [sem(f"w_masked{k}") for k in range(2)]
        w_turned = [sem(f"w_turned{k}") for k in range(2)]
        cols1_ready = sem("cols1_ready")
        cols2_ready = sem("cols2_ready")
        ga_ready = sem("ga_ready")
        gb_ready = sem("gb_ready")
        bounds_in = sem("bounds_in")
        bounds_out = sem("bounds_out")
        dve_step = sem("dve_step")
        pool_step = sem("pool_step")
        x_loaded = [sem(f"x_loaded{k}") for k in range(2)]
        mv_done = [sem(f"mv_done{k}") for k in range(2)]
        ve_done = [sem(f"ve_done{k}") for k in range(2)]
        rstd_done = [sem(f"rstd_done{k}") for k in range(2)]
        z_done = [sem(f"z_done{k}") for k in range(2)]
        t_done = [sem(f"t_done{k}") for k in range(2)]
        hT1_ready = sem("hT1_ready")
        x_copied = sem("x_copied")
        xg_ready = sem("xg_ready")
        attn_done = sem("attn_done")
        pair_free = sem("pair_free")
        x1_ready = sem("x1_ready")
        x1_stored = [sem(f"x1_stored{k}") for k in range(2)]
        hf_ready = sem("hf_ready")
        hi_ready = sem("hi_ready")
        lo_ready = sem("lo_ready")
        h_stored = [sem(f"h_stored{k}") for k in range(2)]
        unit_loaded = [sem(f"unit_loaded{k}") for k in range(NS)]
        unit_turned = sem("unit_turned")
        unit_cast = sem("unit_cast")
        dn_loaded = [sem(f"dn_loaded{k}") for k in range(2)]
        dn_turned = sem("dn_turned")
        dn_cast = sem("dn_cast")
        ht_loaded = sem("ht_loaded")
        gu_done = sem("gu_done")
        silu_done = sem("silu_done")
        h2_done = sem("h2_done")
        h2hi_done = sem("h2hi_done")
        down_done = sem("down_done")
        down_read = sem("down_read")
        tmp_ready = sem("tmp_ready")
        scaled = sem("scaled")
        res_ready = sem("res_ready")
        x1_loaded = [sem(f"x1_loaded{k}") for k in range(4)]
        res_stored = [sem(f"res_stored{k}") for k in range(4)]

        SLOT = [0, 1, 2] * 3 + [3, 4, 5]
        PIECE_COUNT = [16 * (m // NM + 1) for m in range(3 * NM)] + [16] * 3
        DVE_SUMMED = {0: 2, 2: 4, 4: 5, 5: 6, 6: 8, 8: 10, 10: 11, 11: 12}
        POOL_SUMMED = {1: 2, 3: 4, 7: 6, 9: 8}
        UNIT_INC = 16 * A
        ND = FC * (D // P) + 1
        GU = sum(UNITS_AFTER)
        assert GU % 2 == 0 and (ND - 1) % GU == 0

        def dn_unit(j, i):
            return GU // FC * j + i // FC, i % FC

        primed = (h2_done, res_ready, dn_turned, dn_cast, down_read)
        PRIMED = 1
        NCONST = 12
        block = ctx.enter_context(nc.Block())

        class Tile:
            def __init__(self, j, o):
                self.j, self.o = j, o
                self.n, self.half, self.par = 2 * j + o, j + o // 2, o % 2

            def __add__(self, d):
                return Tile(self.j, self.o + d)

        LAST = NT - 1
        FIRST_LOOPED, PAIRS = 5, (NT - 8) // 2

        def static(t, lo, hi):
            return not isinstance(t.n, int) or lo <= t.n <= hi

        def each_tile(eng, step, first=0):
            for i in range(first, FIRST_LOOPED):
                step(Tile(0, i))
            with eng.Fori(0, PAIRS) as j:
                step(Tile(j, FIRST_LOOPED))
                step(Tile(j, FIRST_LOOPED + 1))
            for i in range(FIRST_LOOPED + 2 * PAIRS, NT + 1):
                step(Tile(0, i))

        def units(t):
            if static(t, 2, LAST):
                for s in range(NS):
                    r = NS * (t.o - 2) + s
                    yield s, 2 * NS * t.j + r, NS * t.j + r // 2, r % 2

        LAST_UNIT = [(0, 2 * FT, FT, 0)]
        NU = 2 * FT + 1
        assert NS * (NT - 2) == 2 * FT

        def trailing(t):
            if not isinstance(t.n, int) or t.n > 4:
                return [t + (-2)]
            return {3: [Tile(0, 0)], 4: [Tile(0, 1), Tile(0, 2)]}.get(t.n, [])

        def mask_quarter(eng, q):
            w = wst[q % 2].rearrange("p (b i) -> p b i", i=Q)
            bits = msum[q].rearrange("p (b o) -> p b o", o=1).to_broadcast([P, QB * KT, Q])
            eng.tensor_tensor(w, w, bits, ALU.mult).then_inc(w_masked[q % 2], 1)

        def halves_of(v, h, src):
            if v in (2, 5):
                return [(acc[v][:, h * H:(h + 1) * H], src)]
            by_tile = acc[v].rearrange("p (c a i) -> p a c i", c=KT, a=A)
            return [(by_tile[:, 2 * h + k], src[:, k * KA:(k + 1) * KA].rearrange("p (c i) -> p c i", c=KT))
                    for k in range(A // 2)]

        def wait_summed(eng, m):
            if m in DVE_SUMMED:
                eng.wait_ge(dve_summed, DVE_SUMMED[m])
            else:
                eng.wait_ge(pool_summed, POOL_SUMMED[m])

        @block.sync
        def _(sp):
            def load_x(t):
                sp.dma_start(xt[t.par], x_v[t.n]).then_inc(x_loaded[t.par], 16)

            def load_piece(m):
                if NM <= m < 3 * NM:
                    wait_summed(sp, m - NM)
                elif m == 3 * NM:
                    sp.wait_ge(mask_summed, NQ)
                dst = mp[SLOT[m]].rearrange("p (t n) -> p t n", t=KT)
                sp.dma_start(dst, mod_v[:, :, m * H:(m + 1) * H]).then_inc(piece_loaded[SLOT[m]], 16)

            def load_units(t, todo=None):
                for s, u, c, g in todo or units(t):
                    if static(t, 3, NT):
                        sp.wait_ge(unit_turned, u - NS + 1)
                    dst = stg[s].rearrange("p (b k) -> p b k", b=A)
                    for a in range(A):
                        rows = slice(Q * a, Q * (a + 1))
                        if isinstance(c, int) and c == FT:
                            for gg in range(2):
                                sp.dma_start(dst[rows, 2 * gg:2 * gg + 2], gu_l[gg][a]).then_inc(unit_loaded[s], 16)
                        else:
                            sp.dma_start(dst[rows], gu_v[g][c, a]).then_inc(unit_loaded[s], 16)

            def load_mask(q):
                if q >= 2:
                    sp.wait_ge(mask_summed, q - 1)
                for a in range(A):
                    sp.dma_start(mst[q % 2].rearrange("p (b k) -> p b k", b=QB)[Q * a:Q * (a + 1)], m_v[q, a])\
                      .then_inc(m_loaded[q % 2], 16)

            def load_weight(q):
                if q >= 2:
                    sp.wait_ge(w_turned[q % 2], 1)
                for a in range(A):
                    sp.dma_start(wst[q % 2].rearrange("p (b k) -> p b k", b=QB)[Q * a:Q * (a + 1)], w_v[q, a])\
                      .then_inc(w_loaded[q % 2], 16)

            sp.wait_ge(consts_set, 1)
            sp.dma_start(cvec, c_in.rearrange("o (p t) -> (o p) t", p=P)).then_inc(c_loaded, 16)
            load_x(Tile(0, 0))
            load_piece(0)
            load_piece(1)
            load_x(Tile(0, 1))
            load_piece(2)
            load_piece(3)
            for pair in range(NQ // 2):
                for q in (2 * pair, 2 * pair + 1):
                    load_mask(q)
                for q in (2 * pair, 2 * pair + 1):
                    load_weight(q)
            load_piece(4)
            load_piece(5)
            for i in range(2):
                sp.wait_ge(x_copied, i + 1)
                sp.wait_ge(z_done[0], i + 1)
                load_x(Tile(0, i + 2))
            for m in range(6, 10):
                load_piece(m)

            def step(t):
                if static(t, 1, LAST - 3):
                    sp.wait_ge(z_done[0], t.n + 2)
                    sp.wait_ge(xg_ready, t.n + 2)
                    load_x(t + 3)
                if static(t, 1, LAST - 1):
                    load_units(t + 1)
                if isinstance(t.n, int) and t.n == LAST:
                    load_units(t, LAST_UNIT)

            each_tile(sp, step, 1)

            def load_h(b, ts):
                for t in ts:
                    sp.dma_start(hT_in[:, t], h_blk[b, :, t]).then_inc(ht_loaded, 16)

            for k in range(2):
                sp.wait_ge(h_stored[k], 16 * (BT // 2))
            sp.wait_ge(xg_ready, NT)
            load_h(0, [0])
            sp.wait_ge(unit_turned, NU - 1)
            load_h(0, [2, 3])
            sp.wait_ge(unit_turned, NU)
            load_h(0, [1])
            sp.wait_ge(attn_done, NT)
            sp.wait_ge(z_done[0], NT)
            load_piece(10)
            load_piece(11)
            sp.wait_ge(t_done[0], NT)
            sp.dma_start(down_s_row, down_s.rearrange("n o -> o n").to_broadcast([P, D])).then_inc(down_s_loaded, 16)
            sp.wait_ge(unit_cast, NU)

            def load_dn(j, i):
                dq, fq = dn_unit(j, i)
                if not isinstance(j, int) or j or i >= 2:
                    sp.wait_ge(dn_turned, GU * j + i - 1 + PRIMED)
                for a in range(A):
                    dst = dstg[i % 2][Q * a:Q * (a + 1)].rearrange("p (b k) -> p b k", b=A)
                    sp.dma_start(dst, dn_v[dq, fq, a]).then_inc(dn_loaded[i % 2], 16)

            with sp.Fori(0, ND // GU) as j:
                for i in range(GU):
                    load_dn(j, i)
            sp.wait_ge(dn_turned, ND - 1 + PRIMED)
            for a in range(A):
                dst = dlast[Q * a:Q * (a + 1), :].rearrange("p (b k) -> p b k", k=Q)
                sp.dma_start(dst, dn_l[a % 2]).then_inc(dn_loaded[0], 16)
            sp.wait_ge(dn_cast, ND + PRIMED)

            G = 2 * BT

            def load_x1(b, g):
                if not isinstance(b, int) or b or g >= 4:
                    sp.wait_ge(res_stored[g % 4], 32 * b + 16 * (g // 4))
                sp.dma_start(io[g % 4], x1_d[BT * b + g // 2, :, (g % 2) * H:(g % 2 + 1) * H])\
                  .then_inc(x1_loaded[g % 4], 16)

            def store_block(b, last):
                for k in range(2):
                    sp.wait_ge(x1_stored[k], 16 * NT // 2)
                for g in range(4):
                    load_x1(b, g)
                if not last:
                    sp.wait_ge(gu_done, NF * b + NF)
                    for k in range(2):
                        sp.wait_ge(h_stored[k], 16 * NT // 2)
                    load_h(b + 1, range(BT))
                for g in range(G):
                    sp.wait_ge(res_ready, G * b + g + 1 + PRIMED)
                    sp.dma_start(out_v[BT * b + g // 2, :, (g % 2) * H:(g % 2 + 1) * H], io[g % 4])\
                      .then_inc(res_stored[g % 4], 16)
                    if g < 4:
                        load_x1(b, g + 4)

            store_block(0, False)
            with sp.Fori(1, NB - 1) as b:
                store_block(b, False)
            store_block(NB - 1, True)
            for k in range(4):
                sp.wait_ge(res_stored[k], 16 * (2 * NT // 4))

        @block.gpsimd
        def _(pool):
            pool.memset(small[:, :], 0.0).then_inc(consts_set, 1)
            pool.memset(ident, 0.0).then_inc(consts_set, 1)
            pool.memset(blk1, 0.0).then_inc(consts_set, 1)
            pool.wait_ge(consts_set, 3)
            pool.affine_select(out=ident, in_=ident, compare_op=ALU.not_equal, fill=1.0, base=0,
                               pattern=[[-1, P]], channel_multiplier=1).then_inc(consts_set, 1)
            for a in range(A):
                r = slice(Q * a, Q * (a + 1))
                pool.wait_ge(consts_set, 4 + a)
                pool.memset(blk1[r, r], 1.0).then_inc(consts_set, 1)
            pool.wait_ge(consts_set, 8)
            for v, value in ((mhalf, -0.5), (eps, EPS), (one, 1.0), (two, 2.0)):
                pool.memset(v, value).then_inc(consts_set, 1)
            pool.wait_ge(consts_set, NCONST)
            for k, s in enumerate(primed):
                pool.memset(spare[:, k:k + 1], 0.0).then_inc(s, PRIMED)

            steps = [0]

            def link(*ins):
                for i in ins:
                    i.then_inc(pool_step, 1)
                steps[0] += len(ins)
                pool.wait_ge(pool_step, steps[0])

            def rstd_of(L, n):
                pool.wait_ge(mv_done[L], n + 1)
                pool.tensor_tensor(ve[L], mv[L][:, 1:2], eps, ALU.add).then_inc(ve_done[L], 1)
                pool.wait_ge(ve_done[L], n + 1)
                pool.tensor_tensor(rstd[L], ve[L], mhalf, ALU.pow).then_inc(rstd_done[L], 1)

            def add_bias(t):
                pool.wait_ge(x_loaded[t.par], 16 * t.half + 16)
                pool.tensor_tensor(xg[t.par], xt[t.par], gab, ALU.add).then_inc(xg_ready, 1)

            rstd_of(0, 0)
            pool.tensor_copy(xg[0], xt[0]).then_inc(x_copied, 1)
            rstd_of(0, 1)
            pool.tensor_copy(xg[1], xt[1]).then_inc(x_copied, 1)

            def sum_right(v):
                pool.wait_ge(piece_scaled, {0: 1, 1: 2, 3: 3, 4: 4}[v])
                if v in (3, 4):
                    pool.wait_ge(acc_used, v - 1)
                w = mp[SLOT[2 * v + 1]].rearrange("p (t n) -> p t n", t=KT)
                n = KT // 2
                while n > 1:
                    link(pool.tensor_tensor(w[:, 0:n], w[:, 0:n], w[:, n:2 * n], ALU.add))
                    n //= 2
                for (dst, a), (_, b) in zip(halves_of(v, 1, w[:, 0]), halves_of(v, 1, w[:, 1])):
                    pool.tensor_tensor(dst, a, b, ALU.add).then_inc(pool_summed, 1)

            sum_right(0)
            sum_right(1)
            for q in range(0, NQ, 2):
                pool.wait_ge(mask_bits, q + 1)
                pool.wait_ge(w_loaded[0], A * 16 * (q // 2 + 1))
                mask_quarter(pool, q)

            def lo_part(r):
                pool.wait_ge(hi_ready, r.n + 1)
                pool.tensor_tensor(hs[r.par][:, 1, :], hf, hs[r.par][:, 0, :], ALU.subtract).then_inc(lo_ready, 1)
                pool.wait_ge(lo_ready, r.n + 1)
                pool.dma_start(h_d[r.n], hs[r.par].rearrange("p s e -> p (s e)")).then_inc(h_stored[r.par], 16)

            rstd_of(0, 2)

            def step(t):
                tile = t.n if isinstance(t.n, int) else None
                early = tile in range(FIRST_LOOPED - 1)
                if static(t, FIRST_LOOPED, LAST - 2):
                    rstd_of(0, t.n + 2)
                if tile in (1, 2):
                    sum_right(tile + 2)
                if tile == 0:
                    pool.wait_ge(ga_ready, 1)
                    pool.wait_ge(x_copied, 2)
                    for i in range(2):
                        pool.tensor_tensor(xg[i], xg[i], gab, ALU.add).then_inc(xg_ready, 1)
                for r in trailing(t):
                    lo_part(r)
                if static(t, 0, LAST):
                    rstd_of(1, t.n)
                if early:
                    rstd_of(0, t.n + 3)
                if tile == 2:
                    pool.wait_ge(bounds_in, 4)
                    pool.partition_all_reduce(bma, bmx, P, bass.bass_isa.ReduceOp.max).then_inc(bounds_out, 1)
                if static(t, 0, LAST):
                    pool.wait_ge(x1_ready, t.n + 1)
                if static(t, 0, LAST - 2):
                    add_bias(t + 2)
                if static(t, 0, LAST):
                    pool.dma_start(x1_d[t.n], x1[t.par]).then_inc(x1_stored[t.par], 16)

            each_tile(pool, step)
            lo_part(Tile(0, LAST))

        @block.scalar
        def _(act):
            act.wait_ge(consts_set, NCONST)
            act.wait_ge(c_loaded, 16)
            act.activation(csil, cvec, ACT.Silu).then_inc(silu_c_done, 1)

            def scale_right(v):
                m = 2 * v + 1
                act.wait_ge(piece_loaded[SLOT[m]], PIECE_COUNT[m])
                w = mp[SLOT[m]].rearrange("p (t n) -> p t n", t=KT)
                for t in range(KT):
                    last = act.activation(w[:, t], w[:, t], ACT.Copy, scale=csil[:, t:t + 1])
                last.then_inc(piece_scaled, 1)

            act.wait_ge(silu_c_done, 1)
            scale_right(0)
            scale_right(1)
            act.wait_ge(acc_used, 2)
            act.activation(colm[:, 0:KT], colp[:, 0:KT], ACT.Copy).then_inc(cols1_ready, 1)
            act.activation(colm[:, KT:2 * KT], colp[:, KT:2 * KT], ACT.Copy, bias=1.0).then_inc(cols1_ready, 1)
            act.wait_ge(cols1_ready, 2)

            def shift_scale(dst, src, L):
                for c in range(KT):
                    last = act.activation(dst[:, c, :], src[:, c, :], ACT.Identity,
                                          scale=colm[:, (2 * L + 1) * KT + c:(2 * L + 1) * KT + c + 1],
                                          bias=colm[:, 2 * L * KT + c:2 * L * KT + c + 1])
                return last

            z1T_c = z1T.rearrange("p h (c t) -> p (h c) t", t=P)
            z2T_c = z2T.rearrange("p h (c t) -> p (h c) t", t=P)
            hf_c = hf.rearrange("p (c t) -> p c t", c=KT)

            def turn_out(t):
                act.wait_ge(t_done[0], t.n + 1)
                if static(t, 2, NT):
                    act.wait_ge(attn_done, t.n - 1)
                shift_scale(hT1[t.par], z1T_c, 0).then_inc(hT1_ready, 1)

            turn_out(Tile(0, 0))

            def load_scales():
                act.dma_start(gab, bias.rearrange("(o n) -> o n", o=1).to_broadcast([P, D])).then_inc(bias_loaded, 16)
                for s_in, s_col, r in ((gate_s, sgs, 0), (up_s, sus, P // 2)):
                    for a in range(A):
                        src = s_in[FA * a:FA * (a + 1), :].rearrange("(c i) o -> i (c o)", i=Q)
                        act.dma_start(s_col[Q * a:Q * (a + 1), 0:FT], src).then_inc(scales_loaded, 16)
                    act.dma_start(s_col[r:r + FL, FT:NF], s_in[FT * P:F, :]).then_inc(scales_loaded, 16)

            def cast_units(t, todo=None):
                for s, u, c, g in todo or units(t):
                    act.wait_ge(unit_turned, u + 1)
                    act.activation(wgu_u[:, 2 * c + g, :], trn[s], ACT.Copy).then_inc(unit_cast, 1)

            def second_input(r):
                act.wait_ge(t_done[1], r.n + 1)
                if static(r, 1, NT):
                    act.wait_ge(lo_ready, r.n)
                shift_scale(hf_c, z2T_c, 1).then_inc(hf_ready, 1)
                act.wait_ge(hf_ready, r.n + 1)
                if static(r, 2, NT):
                    act.wait_ge(h_stored[r.par], 16 * r.half)
                act.activation(hs[r.par][:, 0, :], hf, ACT.Copy).then_inc(hi_ready, 1)

            def step(t):
                tile = t.n if isinstance(t.n, int) else None
                if static(t, 0, LAST - 1):
                    turn_out(t + 1)
                if tile == 0:
                    wait_summed(act, 4)
                    load_scales()
                if tile in (1, 2):
                    scale_right(tile + 2)
                if tile == 2:
                    for k in range(2):
                        act.wait_ge(w_turned[k], NQ // 2)
                elif tile == 3:
                    act.wait_ge(cols2_ready, 2)
                    second_input(Tile(0, 0))
                    cast_units(Tile(0, 2))
                elif tile == 4:
                    second_input(Tile(0, 1))
                    cast_units(Tile(0, 3))
                    second_input(Tile(0, 2))
                    wait_summed(act, 9)
                    cast_units(t)
                else:
                    cast_units(t)
                    for r in trailing(t):
                        second_input(r)
                    if tile == LAST:
                        cast_units(t, LAST_UNIT)

            each_tile(act, step)

            def tile_out(n, c, k):
                act.wait_ge(gu_done, n + 1)
                act.wait_ge(h2_done, n + PRIMED)
                act.activation(silu, pA[:, 2 * k, :], ACT.Silu, scale=sgs[:, bass.ds(c, 1)]).then_inc(silu_done, 1)
                act.wait_ge(h2_done, n + 1 + PRIMED)
                act.activation(h2[:, 0, c, :], pA[:, 2 * k + 1, :], ACT.Copy, scale=1.0 / LO).then_inc(h2hi_done, 1)

            def last_tile_out(n):
                k, lo_h, up_h = 2 * ((NF - 1) % 2), slice(0, FL), slice(FL, P)
                act.wait_ge(gu_done, n + 1)
                act.wait_ge(h2_done, n + PRIMED)
                act.activation(silu[up_h], pA[lo_h, k, :], ACT.Silu, scale=sgs[lo_h, FT:NF]).then_inc(silu_done, 1)
                act.wait_ge(h2_done, n + 1 + PRIMED)
                act.activation(h2[lo_h, 0, FT, :], pA[up_h, k, :], ACT.Copy, scale=1.0 / LO)
                act.activation(h2[up_h, 0, FT, :], pA[up_h, k, :], ACT.Copy, scale=1.0 / LO).then_inc(h2hi_done, 1)

            def dn_out(j, i):
                dq, fq = dn_unit(j, i)
                act.wait_ge(dn_turned, GU * j + i + 1 + PRIMED)
                dst = wd[:, CF * fq:CF * (fq + 1), bass.ds(P * dq, P)]
                act.activation(dst, dtrn.rearrange("p (c d) -> p c d", c=CF), ACT.Copy).then_inc(dn_cast, 1)

            def last_dn_out():
                act.wait_ge(dn_turned, ND + PRIMED)
                act.activation(wd[0:FL, FT, :], dlast_trn[0:FL, :], ACT.Copy)
                act.activation(wd[FL:P, FT, :], dlast_trn[FL:P, :], ACT.Copy, scale=1.0 / LO).then_inc(dn_cast, 1)

            def out_half(q, k):
                act.wait_ge(down_done, q + 1)
                act.wait_ge(res_ready, q + PRIMED)
                act.activation(tmp, pB[:, 2 * k, :], ACT.Copy).then_inc(tmp_ready, 1)

            def down_out(b):
                with act.Fori(0, BT) as ts:
                    for k in range(2):
                        out_half(2 * BT * b + 2 * ts + k, k)

            tile_out(0, 0, 0)
            second_input(Tile(0, LAST))
            tile_out(1, 1, 1)
            tile_out(2, 2, 0)
            for k in range(2):
                act.wait_ge(x1_stored[k], 16 * NT // 2)
                act.wait_ge(h_stored[k], 16 * NT // 2)
            act.wait_ge(gb_ready, 1)
            with act.Fori(0, ND // GU) as j:
                i = 0
                for k, count in enumerate(UNITS_AFTER):
                    tile_out(4 * j + FIRST_DN + k, 4 * j + FIRST_DN + k, (FIRST_DN + k) % 2)
                    for _ in range(count):
                        dn_out(j, i)
                        i += 1
            for c in range(4 * (ND // GU) + FIRST_DN, FT - 1):
                tile_out(c, c, c % 2)
            last_dn_out()
            tile_out(FT - 1, FT - 1, 0)
            last_tile_out(FT)
            down_out(0)
            with act.Fori(1, NB) as b:
                with act.Fori(0, FT // 2) as j:
                    for k in range(2):
                        tile_out(NF * b + 2 * j + k, 2 * j + k, k)
                tile_out(NF * b + FT - 1, FT - 1, 0)
                last_tile_out(NF * b + FT)
                down_out(b)

        @block.tensor
        def _(pe):
            def transpose(L, t):
                z, dst, taken = ((z1, z1T, hT1_ready), (z2, z2T, hf_ready))[L]
                zc = z.rearrange("p (c k) -> p c k", c=KT)
                pe.wait_ge(z_done[L], t.n + 1)
                if static(t, 1, NT):
                    pe.wait_ge(taken, t.n)
                for c in range(KT):
                    last = pe.transpose(dst[:, c // 4, (c % 4) * P:(c % 4 + 1) * P], zc[:, c], ident)
                last.then_inc(t_done[L], 1)

            def attend(t, h, ks=range(KT)):
                if h == 0:
                    pe.wait_ge(hT1_ready, t.n + 1)
                    if static(t, 2, NT):
                        pe.wait_ge(pair_free, t.n - 1)
                for c in ks:
                    last = pe.matmul(pA[:, 2 * t.par + h, :], hT1[t.par][:, c, :], wT[:, c, h * H:(h + 1) * H],
                                     start=(c == 0), stop=(c == KT - 1))
                if h == 1:
                    last.then_inc(attn_done, 1)

            def columns(v, dst):
                for h in range(2):
                    wait_summed(pe, 2 * v + h)
                for c in range(KT):
                    last = pe.matmul(dst[:, c:c + 1], acc[v][:, P * c:P * (c + 1)], one, start=True, stop=True)
                last.then_inc(acc_used, 1)

            def gate_row(v, dst):
                for h in range(2):
                    wait_summed(pe, 2 * v + h)
                for h in range(2):
                    last = pe.matmul(dst[:, h * H:(h + 1) * H], two.to_broadcast([P, P]), acc[v][:, h * H:(h + 1) * H],
                                     start=True, stop=True)
                last.then_inc(acc_used, 1)

            def mask_total_of(q):
                pe.wait_ge(mask_summed, q + 1)
                pe.matmul(sump[q], blk1, msum[q], start=True, stop=True).then_inc(mask_total, 1)

            pe.wait_ge(consts_set, NCONST)
            transpose(0, Tile(0, 0))
            columns(0, colp[:, 0:KT])
            mask_total_of(0)
            mask_total_of(1)
            columns(1, colp[:, KT:2 * KT])
            for k in range(2):
                pe.wait_ge(w_turned[k], 1)
            attend(Tile(0, 0), 0, range(0, 2))
            mask_total_of(2)
            attend(Tile(0, 0), 0, range(2, 4))
            mask_total_of(3)
            transpose(0, Tile(0, 1))
            attend(Tile(0, 0), 0, range(4, KT))
            attend(Tile(0, 1), 0)
            for k in range(2):
                pe.wait_ge(w_turned[k], 2)
            attend(Tile(0, 0), 1)
            gate_row(2, rowp[0])
            transpose(0, Tile(0, 2))
            attend(Tile(0, 1), 1)

            def step(t):
                tile = t.n if isinstance(t.n, int) else None
                if static(t, 0, LAST):
                    attend(t, 0)
                if static(t, 0, LAST - 1):
                    transpose(0, t + 1)
                if tile == 4:
                    transpose(1, Tile(0, 1))
                elif tile != 3:
                    transpose(1, t + (-2))
                if tile == 4:
                    pe.wait_ge(cols2_copied, 1)
                if static(t, 0, LAST):
                    attend(t, 1)
                if tile == 3:
                    pe.wait_ge(pair_free, 3)
                    for v in (3, 4):
                        columns(v, colp2[:, KT * (v - 3):KT * (v - 2)])
                if tile == 4:
                    transpose(1, Tile(0, 2))

            each_tile(pe, step, 2)

            def gate_up(b, n, c, k):
                pe.wait_ge(ht_loaded, 16 * BT * b + 16 * BT)
                pe.wait_ge(pair_free, NT + n - 1)
                for g in range(2):
                    for kc in range(KT):
                        for s in range(2):
                            last = pe.matmul(pA[:, 2 * k + g, :], wgu_u[:, 2 * c + g, P * kc:P * (kc + 1)], hT[:, s, kc],
                                             start=(kc == 0 and s == 0), stop=(kc == KT - 1 and s == 1))
                last.then_inc(gu_done, 1)

            def last_gate_up(n):
                pe.wait_ge(pair_free, NT + n - 1)
                for kc in range(KT):
                    for s in range(2):
                        last = pe.matmul(pA[:, 2 * ((NF - 1) % 2), :], wgu_u[:, 2 * FT, P * kc:P * (kc + 1)], hT[:, s, kc],
                                         start=(kc == 0 and s == 0), stop=(kc == KT - 1 and s == 1))
                last.then_inc(gu_done, 1)

            def down(b, ts, k):
                q = 2 * BT * b + 2 * ts + k
                pe.wait_ge(pair_free, NT + NF * b + FT)
                for c in range(FT):
                    for s in range(2):
                        pe.matmul(pB[:, 2 * k + s, :], h2[:, s, c, bass.ds(P * ts, P)], wd[:, c, k * H:(k + 1) * H],
                                  start=(c == 0), stop=(c == FT - 1 and s == 1))
                pe.wait_ge(pair_free, NT + NF * b + NF)
                pe.matmul(pB[:, 2 * k, :], h2[:, 0, FT, bass.ds(P * ts, P)], wd[:, FT, k * H:(k + 1) * H],
                          start=False, stop=True).then_inc(down_done, 1)
                pe.wait_ge(down_read, q + PRIMED)

            def ffn_block(b, first):
                pe.wait_ge(unit_cast, NU)
                if first:
                    gate_up(b, 0, 0, 0)
                    transpose(1, Tile(0, LAST))
                    gate_up(b, 1, 1, 1)
                    gate_up(b, 2, 2, 0)
                    gate_row(5, rowp[1])
                    gate_up(b, 3, 3, 1)
                with pe.Fori(2 if first else 0, FT // 2) as j:
                    for k in range(2):
                        gate_up(b, NF * b + 2 * j + k, 2 * j + k, k)
                gate_up(b, NF * b + FT - 1, FT - 1, 0)
                last_gate_up(NF * b + FT)
                pe.wait_ge(hf_ready, NT)
                pe.wait_ge(gb_ready, 1)
                pe.wait_ge(dn_cast, ND + PRIMED)
                with pe.Fori(0, BT) as ts:
                    for k in range(2):
                        down(b, ts, k)

            ffn_block(0, True)
            with pe.Fori(1, NB) as b:
                ffn_block(b, False)

        @block.vector
        def _(dve):
            steps = [0]

            def link(*ins):
                for i in ins:
                    i.then_inc(dve_step, 1)
                steps[0] += len(ins)
                dve.wait_ge(dve_step, steps[0])

            def stats(L, n, src):
                for h in range(2):
                    dve.bn_stats(bnst[L][:, 6 * h:6 * h + 6], src[:, h * H:(h + 1) * H])
                dve.drain()
                dve.bn_aggr(mv[L], bnst[L]).then_inc(mv_done[L], 1)

            def normalise(L, t):
                z, src = ((z1, xt[t.par]), (z2, x1[t.par]))[L]
                dve.wait_ge(rstd_done[L], t.n + 1)
                if static(t, 1, NT):
                    dve.wait_ge(t_done[L], t.n)
                dve.tensor_scalar(z.rearrange("p (c a i) -> p a c i", c=KT, a=A),
                                  src.rearrange("p (a c i) -> p a c i", c=KT, a=A),
                                  mv[L][:, 0:1], rstd[L], ALU.subtract, ALU.mult).then_inc(z_done[L], 1)

            def stats1(t):
                dve.wait_ge(x_loaded[t.par], 16 * t.half + 16)
                stats(0, t.n, xt[t.par])

            def norm1(t):
                stats1(t)
                normalise(0, t)

            def residual(t):
                dve.wait_ge(attn_done, t.n + 1)
                if static(t, 2, NT):
                    dve.wait_ge(x1_stored[t.par], 16 * t.half)
                ps = pA[:, 2 * t.par:2 * t.par + 2, :].rearrange("p h n -> p (h n)")
                dve.tensor_tensor(x1[t.par], ps, ga, ALU.mult).then_inc(pair_free, 1)
                dve.wait_ge(pair_free, t.n + 1)
                dve.wait_ge(xg_ready, t.n + 1)
                dve.tensor_tensor(x1[t.par], x1[t.par], xg[t.par], ALU.add).then_inc(x1_ready, 1)
                dve.wait_ge(x1_ready, t.n + 1)
                stats(1, t.n, x1[t.par])

            def turn_units(t, todo=None):
                for s, u, c, g in todo or units(t):
                    dve.wait_ge(unit_loaded[s], UNIT_INC * (t.n - 1) if not (isinstance(c, int) and c == FT)
                                else UNIT_INC * (NT - 2) + 2 * UNIT_INC)
                    if static(t, 3, NT):
                        dve.wait_ge(unit_cast, u - NS + 1)
                    dve.transpose(trn[s].rearrange("p (c b i) -> p c b i", c=KT, b=A),
                                  stg[s].rearrange("p (b c i) -> p c b i", b=A, c=KT)).then_inc(unit_turned, 1)

            def clamp_gate(dst, tmp_row, src):
                link(dve.tensor_scalar(tmp_row, src, 0.0, -0.5, ALU.is_ge, ALU.add))
                link(dve.tensor_scalar(dst.bitcast(I32), src.bitcast(I32), 0x7FFFFFFF, None, ALU.bitwise_and))
                link(dve.scalar_tensor_tensor(out=dst, in0=dst, scalar=2 * GATE_FLOOR, in1=tmp_row,
                                              op0=ALU.max, op1=ALU.mult))

            def sum_half(v, h):
                m = 2 * v + h
                dve.wait_ge(piece_loaded[SLOT[m]], PIECE_COUNT[m])
                if v in (2, 3, 4):
                    dve.wait_ge(acc_used, v - 1)
                w = mp[SLOT[m]].rearrange("p (t n) -> p t n", t=KT)
                link(*[dve.tensor_scalar(dst, src, csil[:, 0:1], None, ALU.mult) for dst, src in halves_of(v, h, w[:, 0])])
                for t in range(1, KT):
                    sums = [dve.scalar_tensor_tensor(out=dst, in0=src, scalar=csil[:, t:t + 1], in1=dst,
                                                     op0=ALU.mult, op1=ALU.add) for dst, src in halves_of(v, h, w[:, t])]
                    if t < KT - 1:
                        link(*sums)
                for i in sums:
                    i.then_inc(dve_summed, 1)

            def mask_sums(q):
                dve.wait_ge(m_loaded[q % 2], A * 16 * (q // 2 + 1))
                dve.tensor_reduce(msum[q], mst[q % 2].rearrange("p (b i) -> p b i", i=Q), AXX, ALU.add)\
                   .then_inc(mask_summed, 1)

            dve.wait_ge(consts_set, NCONST)
            norm1(Tile(0, 0))
            dve.wait_ge(silu_c_done, 1)
            sum_half(0, 0)
            norm1(Tile(0, 1))
            sum_half(1, 0)

            def mask_of(q):
                dve.wait_ge(mask_total, q + 1)
                dve.tensor_scalar(msum[q], sump[q], 0.0, None, ALU.is_gt).then_inc(mask_bits, 1)

            def turn_quarter(q):
                dve.wait_ge(w_masked[q % 2], q // 2 + 1)
                dve.transpose(wT[:, :, QB * Q * q:QB * Q * (q + 1)].rearrange("p c (b i) -> p c b i", i=Q),
                              wst[q % 2].rearrange("p (b c i) -> p c b i", b=QB, c=KT)).then_inc(w_turned[q % 2], 1)

            for pair in range(NQ // 2):
                even, odd = 2 * pair, 2 * pair + 1
                mask_sums(even)
                mask_sums(odd)
                mask_of(even)
                mask_of(odd)
                dve.wait_ge(mask_bits, odd + 1)
                dve.wait_ge(w_loaded[1], A * 16 * (pair + 1))
                mask_quarter(dve, odd)
                turn_quarter(odd)
                turn_quarter(even)
            for h in range(2):
                sum_half(2, h)

            def gate_a():
                dve.wait_ge(acc_used, 3)
                clamp_gate(ga, x1[1], rowp[0])
                dve.wait_ge(bias_loaded, 16)
                dve.tensor_tensor(gab, gab, ga, ALU.mult).then_inc(ga_ready, 1)
                dve.wait_ge(ga_ready, 1)

            s_b, one_cb = colm[:, 2 * KT:3 * KT], colm[:, 3 * KT:4 * KT]

            def bound_of(k, v):
                m = mag[:, 0:v.shape[1]]
                link(dve.scalar_tensor_tensor(out=m, in0=v, scalar=-1.0, in1=v, op0=ALU.mult, op1=ALU.max))
                dve.tensor_reduce(bmx[:, k:k + 1], m, AXX, ALU.max).then_inc(bounds_in, 1)
                dve.wait_ge(bounds_in, (k + 2) % 4 + 1)

            def cols2():
                dve.wait_ge(acc_used, 5)
                link(dve.tensor_copy(s_b, colp2[:, 0:KT]))
                dve.tensor_scalar(one_cb, colp2[:, KT:2 * KT], 1.0, None, ALU.add).then_inc(cols2_copied, 1)
                dve.wait_ge(cols2_copied, 1)
                bound_of(0, one_cb)
                bound_of(1, s_b)

            def scales():
                dve.wait_ge(bounds_out, 1)

                def power(bound, p, s, inv):
                    link(dve.tensor_scalar(bound, bound, 2.0 ** -60, 2.0 ** 60, ALU.max, ALU.min))
                    link(dve.tensor_scalar(p.bitcast(I32), bound.bitcast(I32), 0x7F800000, None, ALU.bitwise_and))
                    link(dve.tensor_scalar(s.bitcast(I32), p.bitcast(I32), -1.0, float((2 * 127 + 14) << 23),
                                           ALU.mult, ALU.add))
                    link(dve.tensor_scalar(inv, p, 2.0 ** -14, None, ALU.mult))

                link(dve.tensor_scalar(b1, bma[:, 0:1], bma[:, 1:2], float(D) ** 0.5, ALU.add, ALU.mult))
                link(dve.tensor_scalar(g1, b1, float(D) ** 0.5 * W_MAX, None, ALU.mult))
                power(b1, p1, s1, i1)
                link(dve.tensor_scalar(u2, g1, bma[:, 3:4], None, ALU.mult))
                link(dve.tensor_scalar(b2, g1, bma[:, 2:3], u2, ALU.mult, ALU.mult))
                power(b2, p2, s2, i2)
                link(dve.tensor_scalar(s2, s2, LO, None, ALU.mult))
                link(dve.tensor_scalar(sgs, sgs, i1, None, ALU.mult))
                link(dve.tensor_scalar(sus, sus, i1, s2, ALU.mult, ALU.mult))
                dve.tensor_scalar(one_cb, one_cb, s1, None, ALU.mult).then_inc(cols2_ready, 1)
                dve.tensor_scalar(s_b, s_b, s1, None, ALU.mult).then_inc(cols2_ready, 1)

            def gate_b():
                dve.wait_ge(acc_used, 6)
                clamp_gate(gbs[:, :], gb_sign, rowp[1])
                dve.wait_ge(down_s_loaded, 16)
                dve.scalar_tensor_tensor(out=gbs[:, :], in0=gbs[:, :], scalar=i2, in1=down_s_row,
                                         op0=ALU.mult, op1=ALU.mult).then_inc(gb_ready, 1)

            def step(t):
                tile = t.n if isinstance(t.n, int) else None
                late_units = tile in (2, 3, 4)
                if not late_units:
                    turn_units(t)
                if tile == 3:
                    stats1(t + 2)
                    cols2()
                    normalise(0, t + 2)
                    scales()
                    turn_units(Tile(0, 2))
                elif static(t, 0, LAST - 2):
                    norm1(t + 2)
                if tile == 0:
                    gate_a()
                if tile == 2:
                    sum_half(4, 0)
                if static(t, 1, NT):
                    normalise(1, t + (-1))
                if tile == LAST:
                    turn_units(t, LAST_UNIT)
                if static(t, 0, LAST):
                    residual(t)
                if tile in (3, 4):
                    turn_units(t)
                if tile == 1:
                    sum_half(3, 0)
                    dve.wait_ge(scales_loaded, 16 * 2 * (A + 1))
                    bound_of(2, sgs)
                    bound_of(3, sus)

            each_tile(dve, step)

            def tile_out(n, c, k):
                dve.wait_ge(silu_done, n + 1)
                up = pA[:, 2 * k + 1, :]
                dve.scalar_tensor_tensor(out=up, in0=up, scalar=sus[:, bass.ds(c, 1)], in1=silu, op0=ALU.mult, op1=ALU.mult)\
                   .then_inc(h2_done, 1)
                dve.wait_ge(h2_done, n + 1 + PRIMED)
                dve.wait_ge(h2hi_done, n + 1)
                dve.scalar_tensor_tensor(out=h2[:, 1, c, :], in0=h2[:, 0, c, :], scalar=-LO, in1=up,
                                         op0=ALU.mult, op1=ALU.add).then_inc(pair_free, 1)

            def last_tile_out(n):
                up_h = slice(FL, P)
                dve.wait_ge(silu_done, n + 1)
                up = pA[up_h, 2 * ((NF - 1) % 2), :]
                dve.scalar_tensor_tensor(out=up, in0=up, scalar=sus[up_h, FT:NF], in1=silu[up_h], op0=ALU.mult,
                                         op1=ALU.mult).then_inc(h2_done, 1)
                dve.wait_ge(h2_done, n + 1 + PRIMED)
                dve.wait_ge(h2hi_done, n + 1)
                dve.scalar_tensor_tensor(out=h2[up_h, 0, FT, :], in0=h2[up_h, 0, FT, :], scalar=-LO, in1=up,
                                         op0=ALU.mult, op1=ALU.add).then_inc(pair_free, 1)

            def turn_dn(j, i):
                v = GU * j + i
                dve.wait_ge(dn_loaded[i % 2], A * 16 * (GU // 2 * j + i // 2 + 1))
                dve.wait_ge(dn_cast, v + PRIMED)
                dve.transpose(dtrn.rearrange("p (c b i) -> p c b i", c=CF, b=A),
                              dstg[i % 2].rearrange("p (b c i) -> p c b i", b=A, c=CF)).then_inc(dn_turned, 1)

            def down_out(b):
                with dve.Fori(0, BT // 2) as r:
                    for k in range(4):
                        q = 2 * BT * b + 4 * r + k
                        dve.wait_ge(tmp_ready, q + 1)
                        dve.scalar_tensor_tensor(out=tmp, in0=pB[:, 2 * (k % 2) + 1, :], scalar=1.0 / LO, in1=tmp,
                                                 op0=ALU.mult, op1=ALU.add).then_inc(down_read, 1)
                        dve.wait_ge(down_read, q + 1 + PRIMED)
                        dve.tensor_tensor(tmp, tmp, gbs[:, (k % 2) * H:(k % 2 + 1) * H], ALU.mult).then_inc(scaled, 1)
                        dve.wait_ge(scaled, q + 1)
                        dve.wait_ge(x1_loaded[k], 32 * b + 16 * r + 16)
                        dve.tensor_tensor(io[k], tmp, io[k], ALU.add).then_inc(res_ready, 1)

            sum_half(5, 0)
            tile_out(0, 0, 0)
            sum_half(5, 1)
            tile_out(1, 1, 1)
            tile_out(2, 2, 0)
            gate_b()
            with dve.Fori(0, ND // GU) as j:
                i = 0
                for k, count in enumerate(UNITS_AFTER):
                    tile_out(4 * j + FIRST_DN + k, 4 * j + FIRST_DN + k, (FIRST_DN + k) % 2)
                    for _ in range(count):
                        turn_dn(j, i)
                        i += 1
            for c in range(4 * (ND // GU) + FIRST_DN, FT - 1):
                tile_out(c, c, c % 2)
            dve.wait_ge(dn_loaded[0], A * 16 * (ND // 2 + 1))
            dve.wait_ge(dn_cast, ND - 1 + PRIMED)
            dve.transpose(dlast_trn, dlast).then_inc(dn_turned, 1)
            tile_out(FT - 1, FT - 1, 0)
            last_tile_out(FT)
            down_out(0)
            with dve.Fori(1, NB) as b:
                with dve.Fori(0, FT // 2) as j:
                    for k in range(2):
                        tile_out(NF * b + 2 * j + k, 2 * j + k, k)
                tile_out(NF * b + FT - 1, FT - 1, 0)
                last_tile_out(NF * b + FT)
                down_out(b)


_INS = ['L0_attn_data', 'L0_attn_mask', 'L0_attn_weight', 'L0_attn_bias', 'L0_ffn_gate_w', 'L0_ffn_gate_s',
        'L0_ffn_up_w', 'L0_ffn_up_s', 'L0_ffn_down_w', 'L0_ffn_down_s', 'L0_c', 'L0_wmod']


def kernel(**inputs):
    import numpy as np
    import concourse.bacc as bacc
    from concourse.bass_utils import run_bass_kernel_spmd

    nc = bacc.Bacc("TRN2", target_bir_lowering=False, num_devices=1)
    arrays, args = {}, []
    for name in _INS:
        a = np.ascontiguousarray(inputs[name])
        arrays[f"in_{name}"] = a
        args.append(nc.dram_tensor(f"in_{name}", a.shape, mybir.dt.from_np(a.dtype), kind="ExternalInput").ap())
    shape = np.asarray(inputs['L0_attn_data']).shape
    out = nc.dram_tensor("out_0", shape, F32, kind="ExternalOutput").ap()
    adaln_kernel(nc, *args, out)
    r = run_bass_kernel_spmd(nc, [arrays], core_ids=[0])
    return r.results[0]["out_0"]
```
